# Optimizing a Trainium2 kernel written in Bass

```python
import numpy as np
import jax
import jax.numpy as jnp

def _softmax(x, axis=-1):
    return jax.nn.softmax(x, axis=axis)

def _gelu(x):
    return jax.nn.gelu(x, approximate=True)

def _silu(x):
    return jax.nn.silu(x)

def _sigmoid(x):
    return jax.nn.sigmoid(x)

def _layernorm(x, axis=-1, eps=1e-05):
    m = jnp.mean(x, axis=axis, keepdims=True)
    v = jnp.var(x, axis=axis, keepdims=True)
    return (x - m) / jnp.sqrt(v + eps)

def _scatter_add(tgt, idx, src, axis=0):
    return tgt.at[idx].add(src)

def _segment_sum(src, seg, n):
    return jax.ops.segment_sum(src, seg, n)
kernel_name = 'mk_sandwich_d1_jaxref_r8_60c4e7'

def setup_inputs(seed: int=0):
    np.random.seed(seed)
    _w = jnp.asarray

    def _L0_attn_setup():
        import jax, jax.numpy as jnp
        import numpy as np
        N_HEADS = 16
        D_MODEL = 128
        D_HEAD = 64
        MAX_SEQ_LEN = 128

        def _pos_bias(rel_pos_bias, T):
            i = jnp.arange(T)[:, None]
            j = jnp.arange(T)[None, :]
            idx = jnp.clip(MAX_SEQ_LEN - 1 - (i - j), 0, MAX_SEQ_LEN - 1)
            bias = rel_pos_bias[:, idx]
            return jnp.where((j <= i)[None], bias, 0.0)
        key = jax.random.key(seed)
        ks = jax.random.split(key, 7)
        std = np.sqrt(2.0 / (D_MODEL + D_HEAD)).astype(np.float32)
        hd = N_HEADS * D_HEAD
        Wq = jax.random.normal(ks[0], (D_MODEL, hd), jnp.float32) * std
        Wk = jax.random.normal(ks[1], (D_MODEL, hd), jnp.float32) * std
        Wv = jax.random.normal(ks[2], (D_MODEL, hd), jnp.float32) * std
        Wo = jax.random.normal(ks[3], (hd, D_MODEL), jnp.float32) * (1.0 / np.sqrt(hd))
        bo = jnp.zeros((D_MODEL,), jnp.float32)
        rel_pos_bias = jax.random.normal(ks[4], (N_HEADS, MAX_SEQ_LEN), jnp.float32) * 0.02
        x = jax.random.normal(ks[5], (4, 128, D_MODEL), jnp.float32)
        return {'x': x, 'Wq': Wq, 'Wk': Wk, 'Wv': Wv, 'Wo': Wo, 'bo': bo, 'rel_pos_bias': rel_pos_bias}
    _L0_attn_in = _L0_attn_setup()

    def _L0_ffn_setup():
        import jax, jax.numpy as jnp
        import numpy as np
        import math
        N_EMBD = 128
        HIDDEN = 4 * N_EMBD
        N_EXPERTS = 8
        TOP_K = 2
        B, T = (4, 256)

        def new_gelu(x):
            c = math.sqrt(2.0 / math.pi)
            return 0.5 * x * (1.0 + jnp.tanh(c * (x + 0.044715 * x * x * x)))

        def _moe_forward(x, Wfc_s, bfc_s, Wproj_s, bproj_s, Wr, Wfc, bfc, Wproj, bproj):
            Bb, Tt, C = x.shape
            xf = x.reshape(Bb * Tt, C)
            N = Bb * Tt
            shared = new_gelu(xf @ Wfc_s + bfc_s) @ Wproj_s + bproj_s
            logits = xf @ Wr
            probs = jax.nn.softmax(logits, axis=-1)
            topk_p, topk_i = jax.lax.top_k(probs, TOP_K)
            topk_p = topk_p / jnp.sum(topk_p, axis=-1, keepdims=True)
            gate = jnp.zeros((N, N_EXPERTS), dtype=xf.dtype)
            gate = gate.at[jnp.arange(N)[:, None], topk_i].add(topk_p)
            routed = jnp.zeros_like(xf)
            for e in range(N_EXPERTS):
                h = new_gelu(xf @ Wfc[e] + bfc[e]) @ Wproj[e] + bproj[e]
                routed = routed + h * gate[:, e:e + 1]
            return (shared + routed).reshape(Bb, Tt, C)
        key = jax.random.key(seed)
        ks = jax.random.split(key, 10)
        s = 0.02
        return {'x': jax.random.normal(ks[0], (B, T, N_EMBD), dtype=jnp.float32), 'Wfc_s': jax.random.normal(ks[1], (N_EMBD, HIDDEN), dtype=jnp.float32) * s, 'bfc_s': jnp.zeros((HIDDEN,), dtype=jnp.float32), 'Wproj_s': jax.random.normal(ks[2], (HIDDEN, N_EMBD), dtype=jnp.float32) * s, 'bproj_s': jnp.zeros((N_EMBD,), dtype=jnp.float32), 'Wr': jax.random.normal(ks[3], (N_EMBD, N_EXPERTS), dtype=jnp.float32) * s, 'Wfc': jax.random.normal(ks[4], (N_EXPERTS, N_EMBD, HIDDEN), dtype=jnp.float32) * s, 'bfc': jnp.zeros((N_EXPERTS, HIDDEN), dtype=jnp.float32), 'Wproj': jax.random.normal(ks[5], (N_EXPERTS, HIDDEN, N_EMBD), dtype=jnp.float32) * s, 'bproj': jnp.zeros((N_EXPERTS, N_EMBD), dtype=jnp.float32)}
    _L0_ffn_in = _L0_ffn_setup()
    _d = {'L0_attn_x': _L0_attn_in['x'], 'L0_attn_Wq': _L0_attn_in['Wq'], 'L0_attn_Wk': _L0_attn_in['Wk'], 'L0_attn_Wv': _L0_attn_in['Wv'], 'L0_attn_Wo': _L0_attn_in['Wo'], 'L0_attn_bo': _L0_attn_in['bo'], 'L0_attn_rel_pos_bias': _L0_attn_in['rel_pos_bias'], 'L0_ffn_Wfc_s': _L0_ffn_in['Wfc_s'], 'L0_ffn_bfc_s': _L0_ffn_in['bfc_s'], 'L0_ffn_Wproj_s': _L0_ffn_in['Wproj_s'], 'L0_ffn_bproj_s': _L0_ffn_in['bproj_s'], 'L0_ffn_Wr': _L0_ffn_in['Wr'], 'L0_ffn_Wfc': _L0_ffn_in['Wfc'], 'L0_ffn_bfc': _L0_ffn_in['bfc'], 'L0_ffn_Wproj': _L0_ffn_in['Wproj'], 'L0_ffn_bproj': _L0_ffn_in['bproj']}
    _x0 = _d['L0_attn_x']
    _d['L0_attn_x'] = jax.random.normal(jax.random.fold_in(jax.random.key(seed), 1), (2, 1024, 128), dtype=_x0.dtype)
    del _x0
    return _d

def reference(L0_attn_x, L0_attn_Wq, L0_attn_Wk, L0_attn_Wv, L0_attn_Wo, L0_attn_bo, L0_attn_rel_pos_bias, L0_ffn_Wfc_s, L0_ffn_bfc_s, L0_ffn_Wproj_s, L0_ffn_bproj_s, L0_ffn_Wr, L0_ffn_Wfc, L0_ffn_bfc, L0_ffn_Wproj, L0_ffn_bproj):

    def _L0_attn_ref(x, Wq, Wk, Wv, Wo, bo, rel_pos_bias):
        import jax, jax.numpy as jnp
        import numpy as np
        N_HEADS = 16
        D_MODEL = 128
        D_HEAD = 64
        MAX_SEQ_LEN = 128

        def _pos_bias(rel_pos_bias, T):
            i = jnp.arange(T)[:, None]
            j = jnp.arange(T)[None, :]
            idx = jnp.clip(MAX_SEQ_LEN - 1 - (i - j), 0, MAX_SEQ_LEN - 1)
            bias = rel_pos_bias[:, idx]
            return jnp.where((j <= i)[None], bias, 0.0)
        B, T, _ = x.shape
        H, dh = (N_HEADS, D_HEAD)
        q = (x @ Wq).reshape(B, T, H, dh).transpose(0, 2, 1, 3)
        k = (x @ Wk).reshape(B, T, H, dh).transpose(0, 2, 1, 3)
        v = (x @ Wv).reshape(B, T, H, dh).transpose(0, 2, 1, 3)
        logits = jnp.einsum('bhqd,bhkd->bhqk', q, k)
        i = jnp.arange(T)[:, None]
        j = jnp.arange(T)[None, :]
        causal = jnp.where(j > i, -jnp.inf, 0.0)
        logits = logits + causal[None, None] + _pos_bias(rel_pos_bias, T)[None]
        logits = logits / dh
        probs = jax.nn.softmax(logits, axis=-1)
        out = jnp.einsum('bhqk,bhkd->bhqd', probs, v)
        out = out.transpose(0, 2, 1, 3).reshape(B, T, H * dh)
        return out @ Wo + bo

    def _L0_ffn_ref(x, Wfc_s, bfc_s, Wproj_s, bproj_s, Wr, Wfc, bfc, Wproj, bproj):
        import jax, jax.numpy as jnp
        import numpy as np
        import math
        N_EMBD = 128
        HIDDEN = 4 * N_EMBD
        N_EXPERTS = 8
        TOP_K = 2
        B, T = (4, 256)

        def new_gelu(x):
            c = math.sqrt(2.0 / math.pi)
            return 0.5 * x * (1.0 + jnp.tanh(c * (x + 0.044715 * x * x * x)))

        def _moe_forward(x, Wfc_s, bfc_s, Wproj_s, bproj_s, Wr, Wfc, bfc, Wproj, bproj):
            Bb, Tt, C = x.shape
            xf = x.reshape(Bb * Tt, C)
            N = Bb * Tt
            shared = new_gelu(xf @ Wfc_s + bfc_s) @ Wproj_s + bproj_s
            logits = xf @ Wr
            probs = jax.nn.softmax(logits, axis=-1)
            topk_p, topk_i = jax.lax.top_k(probs, TOP_K)
            topk_p = topk_p / jnp.sum(topk_p, axis=-1, keepdims=True)
            gate = jnp.zeros((N, N_EXPERTS), dtype=xf.dtype)
            gate = gate.at[jnp.arange(N)[:, None], topk_i].add(topk_p)
            routed = jnp.zeros_like(xf)
            for e in range(N_EXPERTS):
                h = new_gelu(xf @ Wfc[e] + bfc[e]) @ Wproj[e] + bproj[e]
                routed = routed + h * gate[:, e:e + 1]
            return (shared + routed).reshape(Bb, Tt, C)
        return _moe_forward(x, Wfc_s, bfc_s, Wproj_s, bproj_s, Wr, Wfc, bfc, Wproj, bproj)
    x = L0_attn_x
    x = x + _layernorm(_L0_attn_ref(_layernorm(x, axis=-1), L0_attn_Wq, L0_attn_Wk, L0_attn_Wv, L0_attn_Wo, L0_attn_bo, L0_attn_rel_pos_bias), axis=-1)
    x = x + _layernorm(_L0_ffn_ref(_layernorm(x, axis=-1), L0_ffn_Wfc_s, L0_ffn_bfc_s, L0_ffn_Wproj_s, L0_ffn_bproj_s, L0_ffn_Wr, L0_ffn_Wfc, L0_ffn_bfc, L0_ffn_Wproj, L0_ffn_bproj), axis=-1)
    return x

_drawn_inputs = setup_inputs


def setup_inputs(seed=0):
    import zlib

    import numpy as np

    out = dict(_drawn_inputs(seed))
    spreads = {'L0_attn_bo': (0.0, 0.1),
     'L0_ffn_bfc_s': (0.0, 0.1),
     'L0_ffn_bproj_s': (0.0, 0.1),
     'L0_ffn_bfc': (0.0, 0.1),
     'L0_ffn_bproj': (0.0, 0.1)}
    factors = {'L0_attn_rel_pos_bias': 48.251}
    for name, (base, spread) in spreads.items():
        noise = np.random.default_rng([zlib.crc32(name.encode()), seed]).standard_normal(out[name].shape)
        drawn = base * np.exp(spread * noise) if base else spread * noise
        out[name] = jnp.asarray(drawn.astype(out[name].dtype))
    for name, factor in factors.items():
        out[name] = (out[name] * factor).astype(out[name].dtype)
    return out
```

```python
from contextlib import ExitStack

import concourse.bass as bass
from concourse import mybir


def transformer_block(
    nc: bass.Bass,
    x: bass.AP,
    Wq: bass.AP,
    Wk: bass.AP,
    Wv: bass.AP,
    Wo: bass.AP,
    bo: bass.AP,
    rel_pos_bias: bass.AP,
    Wfc_s: bass.AP,
    bfc_s: bass.AP,
    Wproj_s: bass.AP,
    bproj_s: bass.AP,
    Wr: bass.AP,
    Wfc: bass.AP,
    bfc: bass.AP,
    Wproj: bass.AP,
    bproj: bass.AP,
    out: bass.AP,
):
    f32 = mybir.dt.float32
    f32r = mybir.dt.float32r
    ALU = mybir.AluOpType
    ACT = mybir.ActivationFunctionType
    AX = mybir.AxisListType.X

    P = 128
    B, T, D = x.shape
    H, R = rel_pos_bias.shape
    HD = Wq.shape[1]
    DH = HD // H
    NB = B * T // P
    QB = T // P
    S = B * QB
    CH = 4
    W = CH * P
    NC = QB // CH
    E = Wr.shape[1]
    NE = E + 1
    HID = Wfc_s.shape[1]
    HB = HID // P
    NCH = NB // CH
    EPS = 1e-5
    MASKED = 1e30
    SCALE = -1.0 / DH
    assert (P, D, R, DH, B, NC) == (128, 128, 128, 64, 2, 2)

    LAG = 2
    GROUPS = [1 if i < CH else 2 for i in range(QB)]
    G_UNIT = sum(GROUPS)
    G_HEAD = B * G_UNIT

    def group_of(s, g):
        return (s // QB) * G_UNIT + sum(GROUPS[: s % QB]) + g

    PV_SLOT = {QB * b + CH * c + CH - 1 + LAG + 1: (b, c) for b in range(B) for c in range(NC)}
    WO_SLOT = {s + 1: bc for s, bc in PV_SLOT.items()}
    QK_SLOT = {1: (0, 1, 0), 2: (0, 1, 1), QB + 1: (1, 0, 0), QB + 2: (1, 0, 1)}
    SHARED_ORDER = sorted([*QK_SLOT, *[s % S for s in WO_SLOT]])
    N_SHARED = len(SHARED_ORDER)

    def shared_index(h, s, last):
        k = SHARED_ORDER.index(s)
        carried = SHARED_ORDER.index(min(t % S for t in WO_SLOT if t >= S))
        if isinstance(h, int) and h == 0:
            return NC + k - (k > carried)
        skipped = NC if last and s > QB + 2 else 0
        return h * N_SHARED + NC + k - 1 - skipped

    N_TURN = H * 2 * P // W

    v_dram = nc.dram_tensor("v_scratch", (B * T, HD), f32, kind="Internal").ap()
    bias_dram = nc.dram_tensor("bias_scratch", (H, 3 * P), f32, kind="Internal").ap()

    ctx = ExitStack()
    with ctx:
        def sb(name, shape, dt=f32):
            return ctx.enter_context(nc.sbuf_tensor(name, shape, dt))

        def pb(name, shape):
            return ctx.enter_context(nc.psum_tensor(name, shape, f32))

        def sem(name):
            return ctx.enter_context(nc.semaphore(name))

        x_sb = sb("x_sb", [P, NB, D])
        normed = sb("normed", [P, NB, D])
        acc = sb("acc", [P, NB, D])
        nT_hi = sb("nT_hi", [P, B * T], f32r)
        nT_lo = sb("nT_lo", [P, B * T], f32r)
        wqk = sb("wqk", [P, H, 2 * DH])
        wqk_hi = sb("wqk_hi", [P, 2 * DH], f32r)
        wqk_lo = sb("wqk_lo", [P, 2 * DH], f32r)
        wv = sb("wv", [P, HD])
        wo = sb("wo", [P, H, D])
        bo_rows = sb("bo_rows", [P, D])
        rel = sb("rel", [H, R])
        bias_line = sb("bias_line", [H, 3 * P])
        bias_all = sb("bias_all", [P, H, 2 * P])
        bias_b = [sb(f"bias_{b}", [P, 2 * P]) for b in range(B)]
        q_hl = [sb(f"q_hl{b}", [P, T], f32r) for b in range(B)]
        k_hl = [sb(f"k_hl{b}", [P, 2, T], f32r) for b in range(B)]
        v_raw = [sb(f"v_raw{b}", [P, QB, DH]) for b in range(B)]
        v_hl = [sb(f"v_hl{b}", [P, QB, 2 * DH], f32r) for b in range(B)]
        probs = [sb(f"probs{r}", [P, T]) for r in range(4)]
        pT_hi = [sb(f"pT_hi{c}", [P, CH * (c + 1), W], f32r) for c in range(NC)]
        pT_lo = [sb(f"pT_lo{c}", [P, CH * (c + 1), W], f32r) for c in range(NC)]
        oT = [sb(f"oT{c}", [P, W]) for c in range(NC)]
        far_min = sb("far_min", [P, S])
        row_min = sb("row_min", [P, S])
        row_sum = sb("row_sum", [P, S])
        row_inv = sb("row_inv", [P, S])
        ident = sb("ident", [P, P])
        exchange = sb("exchange", [P, P])
        stats = sb("stats", [P, NB, 6])
        mv = sb("mv", [P, NB, 2])
        var_eps = sb("var_eps", [P, NB])
        std = sb("std", [P, NB])
        newton = sb("newton", [P, NB])
        rstd = sb("rstd", [P, NB])
        wv_hi = pT_hi[1][:, 0:2, :].rearrange("p a b -> p (a b)")
        wv_lo = pT_lo[1][:, 0:2, :].rearrange("p a b -> p (a b)")
        wfc_raw = [sb(f"wfc_raw{i}", [P, HID]) for i in range(2)]
        wfc_hi = [pT_hi[1][:, 2 + i, :] for i in range(2)]
        wfc_lo = [pT_lo[1][:, 2 + i, :] for i in range(2)]
        wproj = [sb(f"wproj{i}", [P, HB, D]) for i in range(2)]
        bfc_rows = sb("bfc_rows", [NE * HB, P])
        bfc_cols = sb("bfc_cols", [P, NE * HB])
        hidden = [[probs[2 * i + j] for j in range(2)] for i in range(2)]
        wr = sb("wr", [P, E])
        wr_hi = sb("wr_hi", [P, E], f32r)
        wr_lo = sb("wr_lo", [P, E], f32r)
        bproj_rows = sb("bproj_rows", [NE, D])
        logit = sb("logit", [P, NB, E])
        rank = sb("rank", [P, NB, E])
        pick = [sb(f"pick{i}", [P, NB, E]) for i in range(2)]
        order = sb("order", [P, E])
        top = [sb(f"top{i}", [P, NB]) for i in range(2)]
        first = sb("first", [P, NB])
        gate = sb("gate", [P, NB, NE])
        gate_T = sb("gate_T", [NE, B * T])

        score_ps = [pb(f"score_ps{r}", [P, T]) for r in range(2)]
        trans_ps = [pb(f"trans_ps{r}", [P, W]) for r in range(2)]
        out_ps = pb("out_ps", [P, W])
        shared_ps = pb("shared_ps", [P, W])
        banks = [score_ps[r // 2][:, (r % 2) * W:(r % 2 + 1) * W] for r in range(4)]

        act_passed = sem("act_passed")
        dve_passed = sem("dve_passed")
        pool_passed = sem("pool_passed")
        x_loaded = sem("x_loaded")
        attn_w_loaded = sem("attn_w_loaded")
        small_loaded = sem("small_loaded")
        bias_line_stored = sem("bias_line_stored")
        bias_loaded = sem("bias_loaded")
        bias_turn_psum = sem("bias_turn_psum")
        bias_turned = sem("bias_turned")
        ident_ready = sem("ident_ready")
        pool_done = sem("pool_done")
        dve_done = sem("dve_done")
        wqk_scaled = sem("wqk_scaled")
        wv_split = sem("wv_split")
        var_ready = sem("var_ready")
        std_ready = sem("std_ready")
        normed_ready = sem("normed_ready")
        nT_psum = sem("nT_psum")
        nT_hi_ready = sem("nT_hi_ready")
        nT_ready = sem("nT_ready")
        v_psum = sem("v_psum")
        v_evac_act = sem("v_evac_act")
        v_evac_dve = sem("v_evac_dve")
        v_stored = [sem(f"v_stored{r}") for r in range(4)]
        zeros_ready = sem("zeros_ready")
        wqk_hi_done = sem("wqk_hi_done")
        wqk_ready = sem("wqk_ready")
        bias_ready = sem("bias_ready")
        v_loaded = [sem(f"v_loaded{b}") for b in range(B)]
        v_hi_done = sem("v_hi_done")
        v_ready = sem("v_ready")
        qk_psum = sem("qk_psum")
        qk_hi = sem("qk_hi")
        k_lo = sem("k_lo")
        k_copied = [sem(f"k_copied{b}") for b in range(B)]
        scores_ready = sem("scores_ready")
        far_ready = sem("far_ready")
        min_ready = sem("min_ready")
        probs_ready = sem("probs_ready")
        pT_psum = sem("pT_psum")
        pT_hi_ready = sem("pT_hi_ready")
        pT_ready = sem("pT_ready")
        inv_ready = sem("inv_ready")
        oT_psum = sem("oT_psum")
        oT_ready = sem("oT_ready")
        wo_psum = sem("wo_psum")
        shared_free = sem("shared_free")
        moe_w_loaded = [sem(f"moe_w_loaded{i}") for i in range(2)]
        wfc_hi_done = sem("wfc_hi_done")
        wfc_ready = sem("wfc_ready")
        wr_ready = sem("wr_ready")
        logit_psum = sem("logit_psum")
        exp_ready = sem("exp_ready")
        logit_ready = sem("logit_ready")
        gate_ready = sem("gate_ready")
        gate_T_psum = sem("gate_T_psum")
        gate_T_ready = sem("gate_T_ready")
        bias_psum = sem("bias_psum")
        bfc_T_psum = sem("bfc_T_psum")
        bfc_ready = sem("bfc_ready")
        fc_psum = sem("fc_psum")
        hidden_ready = sem("hidden_ready")
        moe_psum = sem("moe_psum")
        moe_added = sem("moe_added")
        result_ready = sem("result_ready")
        result_stored = sem("result_stored")

        block = ctx.enter_context(nc.Block())
        x_blocks = x.rearrange("b (t p) d -> p (b t) d", p=P)
        out_blocks = out.rearrange("b (t p) d -> p (b t) d", p=P)

        @block.sync
        def _(sp):
            for c in range(NCH):
                sp.dma_start(x_sb[:, CH * c:CH * (c + 1), :],
                             x_blocks[:, CH * c:CH * (c + 1), :]).then_inc(x_loaded, 16)
            sp.dma_start(wv[:], Wv).then_inc(attn_w_loaded, 16)
            sp.dma_start(wqk[:, :, 0:DH], Wq.rearrange("p (h d) -> p h d", h=H)).then_inc(attn_w_loaded, 16)
            sp.dma_start(wqk[:, :, DH:2 * DH], Wk.rearrange("p (h d) -> p h d", h=H)).then_inc(attn_w_loaded, 16)
            for r in range(2):
                sp.dma_start(wo[r * DH:(r + 1) * DH, :, :],
                             Wo.rearrange("(h d) n -> d h n", h=H)).then_inc(attn_w_loaded, 16)

            sp.wait_ge(dve_done, 3)
            sp.dma_start(bias_dram, bias_line[:]).then_inc(bias_line_stored, 16)
            sp.wait_ge(bias_line_stored, 16)
            sp.dma_start(bias_all[:], bass.AP(bias_dram.tensor, 0, [[1, P], [3 * P, H], [1, 2 * P]]))\
              .then_inc(bias_loaded, 16)

            for t in range(NB):
                sp.wait_ge(v_evac_act, t + 1)
                sp.wait_ge(v_evac_dve, t + 1)
                sp.dma_start(v_dram[t * P:(t + 1) * P, :], probs[t % 4][:]).then_inc(v_stored[t % 4], 16)

            def load_v(h, b):
                src = bass.AP(v_dram.tensor, h * DH + b * T * HD, [[HD, P], [P * HD, QB], [1, DH]])
                sp.dma_start(v_raw[b][:], src).then_inc(v_loaded[b], 16)

            def copy_k(h, b):
                sp.wait_ge(k_lo, h * 2 * B + 2 * b + 2)
                sp.dma_start(k_hl[b][0:DH, :, :].bitcast(f32), k_hl[b][DH:P, :, :].bitcast(f32))\
                  .then_inc(k_copied[b], 16)

            def head(h, last=False):
                if not (isinstance(h, int) and h == 0):
                    sp.wait_ge(v_ready, h * B)
                load_v(h, 1)
                copy_k(h, 1)
                if not last:
                    sp.wait_ge(v_ready, h * B + 1)
                    load_v(h + 1, 0)
                    copy_k(h + 1, 0)

            copy_k(0, 0)
            for r in range(4):
                sp.wait_ge(v_stored[r], 16 * (NB // 4))
            load_v(0, 0)
            head(0)
            with sp.Fori(1, H - 1) as h:
                head(h)
            head(H - 1, last=True)

            def load_expert(i, wf, wp):
                sp.dma_start(wfc_raw[i][:], wf).then_inc(moe_w_loaded[i], 16)
                sp.dma_start(wproj[i][:], wp).then_inc(moe_w_loaded[i], 16)

            load_expert(0, Wfc_s, Wproj_s.rearrange("(k p) n -> p k n", p=P))
            load_expert(1, Wfc[0, :, :], Wproj[0, :, :].rearrange("(k p) n -> p k n", p=P))

            def expert_src(e):
                return (bass.AP(Wfc.tensor, (e - 1) * (D * HID), [[HID, P], [1, HID]]),
                        bass.AP(Wproj.tensor, (e - 1) * (D * HID), [[D, P], [P * D, HB], [1, D]]))

            def reload(e, i):
                sp.wait_ge(moe_psum, (e - 1) * NCH)
                load_expert(i, *expert_src(e))

            with sp.Fori(2, NE - 1, 2) as e:
                reload(e, 0)
                reload(e + 1, 1)
            reload(NE - 1, 0)

            for c in range(NCH):
                sp.wait_ge(result_ready, c + 1)
                sp.dma_start(out_blocks[:, CH * c:CH * (c + 1), :],
                             normed[:, CH * c:CH * (c + 1), :]).then_inc(result_stored, 16)
            sp.wait_ge(result_stored, 16 * NCH)

        @block.gpsimd
        def _(pool):
            own = [0]

            def then_wait(ins):
                own[0] += 1
                ins.then_inc(pool_done, 1)
                pool.wait_ge(pool_done, own[0])

            pool.dma_start(rel[:], rel_pos_bias).then_inc(small_loaded, 16)
            pool.dma_start(bo_rows[:], bass.AP(bo.tensor, 0, [[0, P], [1, D]])).then_inc(small_loaded, 16)
            pool.dma_start(wr[:], Wr).then_inc(small_loaded, 16)
            pool.dma_start(bproj_rows[0:1, :], bproj_s.rearrange("(a n) -> a n", a=1)).then_inc(small_loaded, 16)
            pool.dma_start(bproj_rows[1:NE, :], bproj).then_inc(small_loaded, 16)
            pool.dma_start(bfc_rows[0:HB, :], bfc_s.rearrange("(k p) -> k p", p=P)).then_inc(small_loaded, 16)
            pool.dma_start(bfc_rows[HB:NE * HB, :], bfc.rearrange("e (k p) -> (e k) p", p=P)).then_inc(small_loaded, 16)
            then_wait(pool.memset(ident[:], 0.0))
            pool.affine_select(out=ident[:], in_=ident[:], compare_op=ALU.not_equal, fill=1.0, base=0,
                               pattern=[[-1, P]], channel_multiplier=1).then_inc(ident_ready, 1)
            then_wait(pool.memset(exchange[:], 0.0))
            pool.affine_select(out=exchange[:], in_=exchange[:], compare_op=ALU.not_equal, fill=1.0,
                               base=1 - P, pattern=[[1, P]], channel_multiplier=1).then_inc(ident_ready, 1)
            pool.wait_ge(attn_w_loaded, 16 * 5)
            then_wait(pool.tensor_copy(wv_hi, wv[:]))
            pool.tensor_tensor(wv_lo, wv[:], wv_hi, ALU.subtract).then_inc(wv_split, 1)

            def split_wqk(h):
                pool.sem_inc(pool_passed, 1)
                pool.tensor_copy(wqk_hi[:], wqk[:, h, :]).then_inc(wqk_hi_done, 1)
                pool.wait_ge(wqk_hi_done, h + 1)
                pool.sem_inc(pool_passed, 1)
                pool.tensor_tensor(wqk_lo[:], wqk[:, h, :], wqk_hi[:], ALU.subtract).then_inc(wqk_ready, 1)

            def take_bias(h, b):
                pool.sem_inc(pool_passed, 1)
                pool.tensor_copy(bias_b[b][:], bias_all[:, h, :]).then_inc(bias_ready, 1)

            for c in range(NC):
                for part in (pT_hi, pT_lo):
                    zero = part[c][:, CH * c + CH - 1, (CH - 2) * P:(CH - 1) * P]
                    pool.tensor_scalar(zero, ident[:], 0.0, None, ALU.mult).then_inc(zeros_ready, 1)

            def split_v(h, b):
                n = h * B + b
                pool.wait_ge(v_loaded[b], h * 16 + 16)
                pool.sem_inc(pool_passed, 1)
                pool.tensor_copy(v_hl[b][:, :, 0:DH], v_raw[b][:]).then_inc(v_hi_done, 1)
                pool.wait_ge(v_hi_done, n + 1)
                pool.tensor_tensor(v_hl[b][:, :, DH:2 * DH], v_raw[b][:], v_hl[b][:, :, 0:DH],
                                   ALU.subtract).then_inc(v_ready, 1)

            def head(h, last=False):
                zero = isinstance(h, int) and h == 0
                if not zero:
                    pool.wait_ge(min_ready, h * S)
                take_bias(h, 1)
                if not zero:
                    pool.wait_ge(oT_psum, h * (B * NC))
                split_v(h, 1)
                if last:
                    return
                pool.wait_ge(qk_psum, h * (2 * B) + 2 * B)
                split_wqk(h + 1)
                pool.wait_ge(min_ready, h * S + QB)
                take_bias(h + 1, 0)
                pool.wait_ge(oT_psum, h * (B * NC) + NC)
                split_v(h + 1, 0)

            pool.wait_ge(wqk_scaled, 1)
            pool.wait_ge(bias_turned, N_TURN)
            split_wqk(0)
            take_bias(0, 0)
            split_v(0, 0)
            head(0)
            with pool.Fori(1, H - 1) as h:
                head(h)
            head(H - 1, last=True)

            pool.wait_ge(small_loaded, 16 * 7)
            then_wait(pool.tensor_copy(wr_hi[:], wr[:]))
            pool.tensor_tensor(wr_lo[:], wr[:], wr_hi[:], ALU.subtract).then_inc(wr_ready, 1)

            def split_wfc(e, i):
                pool.wait_ge(moe_w_loaded[i], (e - i) * 16 + 32)
                pool.sem_inc(pool_passed, 1)
                pool.tensor_copy(wfc_hi[i], wfc_raw[i][:]).then_inc(wfc_hi_done, 1)
                pool.wait_ge(wfc_hi_done, e + 1)
                pool.tensor_tensor(wfc_lo[i], wfc_raw[i][:], wfc_hi[i], ALU.subtract).then_inc(wfc_ready, 1)

            pool.wait_ge(oT_psum, H * B * NC)
            split_wfc(0, 0)
            split_wfc(1, 1)

            def resplit(e, i):
                pool.wait_ge(fc_psum, (e - 1) * (NCH * HB))
                split_wfc(e, i)

            with pool.Fori(2, NE - 1, 2) as e:
                resplit(e, 0)
                resplit(e + 1, 1)
            resplit(NE - 1, 0)

        @block.scalar
        def _(act):
            act.wait_ge(var_ready, 1)
            act.activation(std[:], var_eps[:], ACT.Sqrt).then_inc(std_ready, 1)

            def nT_evac(n):
                for c in range(NCH):
                    act.wait_ge(nT_psum, n * NCH + c + 1)
                    act.activation(nT_hi[:, c * W:(c + 1) * W], trans_ps[c % 2][:], ACT.Copy)\
                       .then_inc(nT_hi_ready, 1)

            nT_evac(0)
            for t in range(NB):
                act.wait_ge(v_psum, 2 * t + 1)
                if t >= 4:
                    act.wait_ge(v_stored[t % 4], 16 * (t // 4))
                act.activation(probs[t % 4][:, 0:W], banks[(2 * t) % 4], ACT.Copy).then_inc(v_evac_act, 1)

            bias_flat = bias_all[:].rearrange("p h c -> p (h c)")
            for n in range(N_TURN):
                act.wait_ge(bias_turn_psum, n + 1)
                act.activation(bias_flat[:, n * W:(n + 1) * W], trans_ps[n % 2][:], ACT.Copy)\
                   .then_inc(bias_turned, 1)

            def exp(h, s):
                n = P * (s % QB + 1)
                act.wait_ge(min_ready, h * S + s + 1)
                act.activation(probs[s % 4][:, 0:n], score_ps[s % 2][:, 0:n], ACT.Exp,
                               bias=row_min[:, s:s + 1], scale=-1.0,
                               accum_out=row_sum[:, s:s + 1]).then_inc(probs_ready, 1)

            def split_hi(h, s):
                b, i = divmod(s, QB)
                c, q = divmod(i, CH)
                u = h * (B * NC) + b * NC + c
                if q == 0 and not (isinstance(u, int) and u < NC):
                    act.wait_ge(oT_psum, u - (NC - 1))
                for g in range(GROUPS[i]):
                    k = group_of(s, g)
                    m = min(CH, i + 1 - CH * g)
                    act.wait_ge(pT_psum, h * G_HEAD + k + 1)
                    act.activation(pT_hi[c][:, CH * g:CH * g + m, q * P:(q + 1) * P],
                                   trans_ps[k % 2][:, 0:m * P].rearrange("p (m q) -> p m q", q=P),
                                   ACT.Copy).then_inc(pT_hi_ready, 1)

            def copy_oT(h, b, c):
                act.wait_ge(oT_psum, h * (B * NC) + b * NC + c + 1)
                act.activation(oT[c][:], out_ps[:], ACT.Copy).then_inc(oT_ready, 1)

            def split_qk_hi(h, b, half):
                act.wait_ge(qk_psum, h * (2 * B) + 2 * b + half + 1)
                if not (isinstance(h, int) and h == 0):
                    act.wait_ge(scores_ready, h * S + QB * b + QB - S)
                cols = slice(half * W, (half + 1) * W)
                act.activation(q_hl[b][0:DH, cols], shared_ps[0:DH, :], ACT.Copy)
                act.activation(k_hl[b][DH:P, 0, cols], shared_ps[DH:P, :], ACT.Copy).then_inc(qk_hi, 1)

            def slot(h, s, carried, last):
                if s >= LAG:
                    split_hi(h, s - LAG)
                elif carried:
                    split_hi(h - 1, s - LAG + S)
                if s < S:
                    exp(h, s)
                if s in PV_SLOT:
                    copy_oT(h, *PV_SLOT[s])
                elif carried and s + S in PV_SLOT:
                    copy_oT(h - 1, *PV_SLOT[s + S])
                if s in QK_SLOT:
                    nxt, b, half = QK_SLOT[s]
                    if not (nxt and last):
                        split_qk_hi(h + nxt, b, half)

            for half in range(2):
                split_qk_hi(0, 0, half)
            for s in range(S):
                slot(0, s, False, False)
            with act.Fori(1, H - 1) as h:
                for s in range(S):
                    slot(h, s, True, False)
            for s in range(S):
                slot(H - 1, s, True, True)
            for s in range(S, S + 4):
                if s - LAG < S:
                    split_hi(H - 1, s - LAG)
                if s in PV_SLOT:
                    copy_oT(H - 1, *PV_SLOT[s])

            for n in (2, 3):
                act.wait_ge(var_ready, n)
                act.activation(std[:], var_eps[:], ACT.Sqrt).then_inc(std_ready, 1)
            nT_evac(1)

            act.wait_ge(bfc_T_psum, 1)
            act.activation(bfc_cols[:], shared_ps[:, 0:NE * HB], ACT.Copy).then_inc(bfc_ready, 1)
            act.wait_ge(bfc_ready, 1)
            act.wait_ge(logit_ready, 1)
            act.activation(rank[:], logit[:], ACT.Exp).then_inc(exp_ready, 1)

            def gelu(e, c, i):
                for k in range(HB):
                    act.wait_ge(fc_psum, e * (NCH * HB) + c * HB + k + 1)
                    if k == 0 and not (isinstance(e, int) and e == 0 and c < 2):
                        act.wait_ge(moe_psum, e * NCH + c - 1)
                    act.sem_inc(act_passed, 1)
                    act.activation(hidden[c % 2][k // 2][:, (k % 2) * W:(k % 2 + 1) * W], banks[k],
                                   ACT.Gelu_apprx_tanh, bias=bfc_cols[:, bass.ds(e * HB + k, 1)]).then_inc(hidden_ready, 1)

            for c in range(NCH):
                gelu(0, c, 0)
            with act.Fori(1, NE - 1, 2) as e:
                for c in range(NCH):
                    gelu(e, c, 1)
                for c in range(NCH):
                    gelu(e + 1, c, 0)

            for c in range(NCH):
                act.wait_ge(var_ready, 4 + c)
                act.activation(std[:, CH * c:CH * (c + 1)], var_eps[:, CH * c:CH * (c + 1)], ACT.Sqrt)\
                   .then_inc(std_ready, 1)

        @block.vector
        def _(dve):
            own = [0]

            def then_wait(ins):
                own[0] += 1
                ins.then_inc(dve_done, 1)
                dve.wait_ge(dve_done, own[0])

            dve.wait_ge(small_loaded, 16 * 7)
            then_wait(dve.tensor_scalar(bias_line[:, P:2 * P], rel[:], rel[:, 0:1], SCALE,
                                        ALU.subtract, ALU.mult))
            then_wait(dve.memset(bias_line[:, 0:P], 0.0))
            then_wait(dve.memset(bias_line[:, 2 * P:3 * P], MASKED))

            def moments(src, lo, hi):
                for t in range(lo, hi):
                    last = dve.bn_stats(stats[:, t, :], src[:, t, :])
                then_wait(last)
                for t in range(lo, hi):
                    last = dve.bn_aggr(mv[:, t, :], stats[:, t, :])
                then_wait(last)
                dve.tensor_scalar(var_eps[:, lo:hi], mv[:, lo:hi, 1], EPS, None, ALU.add).then_inc(var_ready, 1)

            def inverse_std(n, lo, hi):
                r, v, t = rstd[:, lo:hi], var_eps[:, lo:hi], newton[:, lo:hi]
                dve.wait_ge(std_ready, n)
                then_wait(dve.reciprocal(r, std[:, lo:hi]))
                then_wait(dve.tensor_tensor(t, r, r, ALU.mult))
                then_wait(dve.tensor_tensor(t, t, v, ALU.mult))
                then_wait(dve.tensor_scalar(t, t, -0.5, 1.5, ALU.mult, ALU.add))
                then_wait(dve.tensor_tensor(r, r, t, ALU.mult))

            def normalise(dst, src, lo, hi, each=None):
                for t in range(lo, hi):
                    last = dve.tensor_scalar(dst[:, t, :], src[:, t, :], mv[:, t, 0:1], rstd[:, t:t + 1],
                                             ALU.subtract, ALU.mult)
                    if each is not None:
                        last.then_inc(each, 1)
                return last

            def nT_evac(n):
                for c in range(NCH):
                    dve.wait_ge(nT_hi_ready, n * NCH + c + 1)
                    dve.tensor_tensor(nT_lo[:, c * W:(c + 1) * W], trans_ps[c % 2][:],
                                      nT_hi[:, c * W:(c + 1) * W], ALU.subtract).then_inc(nT_ready, 1)

            dve.wait_ge(x_loaded, 16 * NCH)
            moments(x_sb, 0, NB)
            inverse_std(1, 0, NB)
            normalise(normed, x_sb, 0, NB, each=normed_ready)
            dve.wait_ge(attn_w_loaded, 16 * 5)
            dve.tensor_scalar(wqk[:, :, 0:DH], wqk[:, :, 0:DH], SCALE, None, ALU.mult).then_inc(wqk_scaled, 1)
            nT_evac(0)
            for t in range(NB):
                dve.wait_ge(v_psum, 2 * t + 2)
                if t >= 4:
                    dve.wait_ge(v_stored[t % 4], 16 * (t // 4))
                dve.tensor_copy(probs[t % 4][:, W:2 * W], banks[(2 * t + 1) % 4]).then_inc(v_evac_dve, 1)
            for t in range(NB):
                last = dve.tensor_copy(acc[:, t, :], bo_rows[:])
            then_wait(last)

            def row_minimum(h, s):
                b, i = divmod(s, QB)
                ps = score_ps[s % 2]
                n, near = P * (i + 1), min(2 * P, P * (i + 1))
                dve.wait_ge(scores_ready, h * S + s + 1)
                if i == 0:
                    dve.wait_ge(bias_ready, h * B + b + 1)
                start = 3e38
                if i >= 2:
                    dve.tensor_reduce(far_min[:, s:s + 1], ps[:, 0:n - near], AX, ALU.min)\
                       .then_inc(far_ready, 1)
                    dve.wait_ge(far_ready, h * (B * (QB - 2)) + b * (QB - 2) + i - 1)
                    start = far_min[:, s:s + 1]
                dve.sem_inc(dve_passed, 1)
                dve.tensor_tensor_reduce(out=ps[:, n - near:n], in0=ps[:, n - near:n],
                                         in1=bias_b[b][:, 2 * P - near:2 * P], scale=1.0, scalar=start,
                                         op0=ALU.add, op1=ALU.min,
                                         accum_out=row_min[:, s:s + 1]).then_inc(min_ready, 1)

            def split_lo(h, s):
                b, i = divmod(s, QB)
                c, q = divmod(i, CH)
                for g in range(GROUPS[i]):
                    k = group_of(s, g)
                    m = min(CH, i + 1 - CH * g)
                    dst = (slice(None), slice(CH * g, CH * g + m), slice(q * P, (q + 1) * P))
                    dve.wait_ge(pT_hi_ready, h * G_HEAD + k + 1)
                    dve.tensor_tensor(pT_lo[c][dst], trans_ps[k % 2][:, 0:m * P].rearrange("p (m q) -> p m q", q=P),
                                      pT_hi[c][dst], ALU.subtract).then_inc(pT_ready, 1)

            def invert_sums(h, b, c):
                s = QB * b + CH * c
                dve.wait_ge(probs_ready, h * S + s + CH)
                dve.reciprocal(row_inv[:, s:s + CH], row_sum[:, s:s + CH]).then_inc(inv_ready, 1)

            def add_head(h, b, c):
                n = h * (B * NC) + b * NC + c + 1
                dve.wait_ge(wo_psum, n)
                dve.wait_ge(inv_ready, n)
                for j in range(CH):
                    t = QB * b + CH * c + j
                    last = dve.scalar_tensor_tensor(out=acc[:, t, :], in0=shared_ps[:, j * P:(j + 1) * P],
                                                    scalar=row_inv[:, t:t + 1], in1=acc[:, t, :],
                                                    op0=ALU.mult, op1=ALU.add)
                last.then_inc(shared_free, 1)

            def split_qk_lo(h, b, half):
                cols = slice(half * W, (half + 1) * W)
                dve.wait_ge(qk_hi, h * (2 * B) + 2 * b + half + 1)
                dve.tensor_tensor(k_hl[b][DH:P, 1, cols], shared_ps[DH:P, :], k_hl[b][DH:P, 0, cols],
                                  ALU.subtract).then_inc(k_lo, 1)
                dve.tensor_tensor(q_hl[b][DH:P, cols], shared_ps[0:DH, :], q_hl[b][0:DH, cols],
                                  ALU.subtract).then_inc(shared_free, 1)

            def slot(h, s, carried, last):
                if s < S:
                    row_minimum(h, s)
                if s >= LAG:
                    split_lo(h, s - LAG)
                elif carried:
                    split_lo(h - 1, s - LAG + S)
                for slots, do in ((PV_SLOT, invert_sums), (WO_SLOT, add_head)):
                    if s in slots:
                        do(h, *slots[s])
                    elif carried and s + S in slots:
                        do(h - 1, *slots[s + S])
                if s in QK_SLOT:
                    nxt, b, half = QK_SLOT[s]
                    if not (nxt and last):
                        split_qk_lo(h + nxt, b, half)

            for half in range(2):
                split_qk_lo(0, 0, half)
            for s in range(S):
                slot(0, s, False, False)
            with dve.Fori(1, H - 1) as h:
                for s in range(S):
                    slot(h, s, True, False)
            for s in range(S):
                slot(H - 1, s, True, True)
            for s in range(S, S + 4):
                if s - LAG < S:
                    split_lo(H - 1, s - LAG)
                if s in PV_SLOT:
                    invert_sums(H - 1, *PV_SLOT[s])
                if s in WO_SLOT:
                    add_head(H - 1, *WO_SLOT[s])
            dve.wait_ge(shared_free, H * N_SHARED)

            moments(acc, 0, NB)
            inverse_std(2, 0, NB)
            then_wait(normalise(normed, acc, 0, NB))
            then_wait(dve.tensor_tensor(x_sb[:], x_sb[:], normed[:], ALU.add))
            moments(x_sb, 0, NB)
            inverse_std(3, 0, NB)
            normalise(normed, x_sb, 0, NB, each=normed_ready)
            nT_evac(1)

            for k in range(E):
                last = dve.memset(order[:, k:k + 1], float(E - k))
            then_wait(last)
            dve.wait_ge(logit_psum, 1)
            lps = out_ps[:, 0:NB * E].rearrange("p (t e) -> p t e", e=E)
            each = lambda a: a.unsqueeze(2).broadcast_to([P, NB, E])
            then_wait(dve.tensor_reduce(top[0][:], lps, AX, ALU.max))
            dve.tensor_tensor(logit[:], lps, each(top[0][:]), ALU.subtract).then_inc(logit_ready, 1)
            dve.wait_ge(exp_ready, 1)
            prefer = order[:].unsqueeze(1).broadcast_to([P, NB, E])
            for i in range(2):
                then_wait(dve.tensor_reduce(top[i][:], rank[:], AX, ALU.max))
                then_wait(dve.tensor_tensor(pick[i][:], rank[:], each(top[i][:]), ALU.is_equal))
                then_wait(dve.tensor_tensor(pick[i][:], pick[i][:], prefer, ALU.mult))
                then_wait(dve.tensor_reduce(first[:], pick[i][:], AX, ALU.max))
                then_wait(dve.tensor_tensor(pick[i][:], pick[i][:], each(first[:]), ALU.is_equal))
                if i == 0:
                    then_wait(dve.scalar_tensor_tensor(
                        out=rank[:].rearrange("p t e -> p (t e)"), in0=pick[0][:].rearrange("p t e -> p (t e)"),
                        scalar=-2.0, in1=rank[:].rearrange("p t e -> p (t e)"), op0=ALU.mult, op1=ALU.add))
            then_wait(dve.tensor_tensor(first[:], top[0][:], top[1][:], ALU.add))
            then_wait(dve.reciprocal(first[:], first[:]))
            for i in range(2):
                then_wait(dve.tensor_tensor(top[i][:], top[i][:], first[:], ALU.mult))
                then_wait(dve.tensor_tensor(pick[i][:], pick[i][:], each(top[i][:]), ALU.mult))
            then_wait(dve.memset(gate[:, :, 0:1], 1.0))
            dve.tensor_tensor(gate[:, :, 1:NE], pick[0][:], pick[1][:], ALU.add).then_inc(gate_ready, 1)

            for c in range(NCH):
                dve.wait_ge(gate_T_psum, c + 1)
                dve.tensor_copy(gate_T[:, c * W:(c + 1) * W], out_ps[0:NE, :]).then_inc(gate_T_ready, 1)
                dve.wait_ge(bias_psum, c + 1)
                dve.tensor_copy(acc[:, CH * c:CH * (c + 1), :],
                                shared_ps[:].rearrange("p (t d) -> p t d", d=D)).then_inc(gate_T_ready, 1)
            dve.wait_ge(gate_T_ready, 2 * NCH)

            def add_expert(e, c):
                dve.wait_ge(moe_psum, e * NCH + c + 1)
                if not (isinstance(e, int) and e == 0):
                    dve.wait_ge(moe_added, e * NCH + c - NCH + 1)
                for j in range(CH):
                    t = CH * c + j
                    last = dve.scalar_tensor_tensor(out=acc[:, t, :], in0=trans_ps[c % 2][:, j * P:(j + 1) * P],
                                                    scalar=gate[:, t, bass.ds(e, 1)], in1=acc[:, t, :],
                                                    op0=ALU.mult, op1=ALU.add)
                last.then_inc(moe_added, 1)

            for c in range(NCH):
                add_expert(0, c)
            with dve.Fori(1, NE - 1) as e:
                for c in range(NCH):
                    add_expert(e, c)
            for c in range(NCH):
                add_expert(NE - 1, c)

            for c in range(NCH):
                lo, hi = CH * c, CH * (c + 1)
                dve.wait_ge(moe_added, (NE - 1) * NCH + c + 1)
                moments(acc, lo, hi)
            for c in range(NCH):
                lo, hi = CH * c, CH * (c + 1)
                inverse_std(4 + c, lo, hi)
                then_wait(normalise(normed, acc, lo, hi))
                dve.tensor_tensor(normed[:, lo:hi, :], normed[:, lo:hi, :], x_sb[:, lo:hi, :], ALU.add)\
                   .then_inc(result_ready, 1)

        @block.tensor
        def _(pe):
            def three(dst, w_hi, w_lo, m_hi, m_lo, start=True, stop=True):
                pe.matmul(dst, w_hi, m_hi, start=start, stop=False)
                pe.matmul(dst, w_hi, m_lo, start=False, stop=False)
                return pe.matmul(dst, w_lo, m_hi, start=False, stop=stop)

            def transposes(n):
                for c in range(NCH):
                    pe.wait_ge(normed_ready, n * NB + CH * (c + 1))
                    if c >= 2:
                        pe.wait_ge(nT_ready, n * NCH + c - 1)
                    for j in range(CH):
                        last = pe.transpose(trans_ps[c % 2][:, j * P:(j + 1) * P], normed[:, CH * c + j, :], ident[:])
                    last.then_inc(nT_psum, 1)

            pe.wait_ge(ident_ready, 1)
            transposes(0)

            pe.wait_ge(wv_split, 1)
            for t in range(NB):
                if t % CH == 0:
                    pe.wait_ge(nT_ready, t // CH + 1)
                for half in range(2):
                    if t >= 2:
                        pe.wait_ge(v_evac_act if half == 0 else v_evac_dve, t - 1)
                    cols, rows = slice(half * W, (half + 1) * W), slice(t * P, (t + 1) * P)
                    three(banks[(2 * t + half) % 4], nT_hi[:, rows], nT_lo[:, rows],
                          wv_hi[:, cols], wv_lo[:, cols]).then_inc(v_psum, 1)

            bias_flat = bias_all[:].rearrange("p h c -> p (h c)")
            pe.wait_ge(bias_loaded, 16)
            pe.wait_ge(ident_ready, 2)
            for n in range(N_TURN):
                if n >= 2:
                    pe.wait_ge(bias_turned, n - 1)
                pe.matmul(trans_ps[n % 2][:], exchange[:], bias_flat[:, n * W:(n + 1) * W],
                          start=True, stop=True).then_inc(bias_turn_psum, 1)

            def project_qk(h, b, half, before):
                pe.wait_ge(wqk_ready, h + 1)
                if not (isinstance(before, int) and before == 0):
                    pe.wait_ge(shared_free, before)
                cols = slice(b * T + half * W, b * T + (half + 1) * W)
                three(shared_ps[:], wqk_hi[:], wqk_lo[:], nT_hi[:, cols], nT_lo[:, cols]).then_inc(qk_psum, 1)

            def scores(h, s):
                b, i = divmod(s, QB)
                if i == 0:
                    pe.wait_ge(k_copied[b], h * 16 + 16)
                if not (isinstance(h, int) and h == 0 and s < 2):
                    pe.wait_ge(probs_ready, h * S + s - 1)
                q = q_hl[b][:, i * P:(i + 1) * P]
                n = P * (i + 1 + (i % CH == 0))
                at = 0
                for end in [n] if n <= W else [W, n]:
                    for part in range(2):
                        last = pe.matmul(score_ps[s % 2][:, at:end], q, k_hl[b][:, part, at:end],
                                         start=part == 0, stop=part == 1)
                    at = end
                last.then_inc(scores_ready, 1)

            def transpose_probs(h, s):
                i = s % QB
                pe.wait_ge(probs_ready, h * S + s + 1)
                for g in range(GROUPS[i]):
                    k = group_of(s, g)
                    if not (isinstance(h, int) and h == 0 and k < 2):
                        pe.wait_ge(pT_ready, h * G_HEAD + k - 1)
                    for j in range(CH * g, min(CH * (g + 1), i + 1)):
                        o = (j - CH * g) * P
                        last = pe.transpose(trans_ps[k % 2][:, o:o + P], probs[s % 4][:, j * P:(j + 1) * P], ident[:])
                    last.then_inc(pT_psum, 1)

            def values(h, b, c):
                u = h * (B * NC) + b * NC + c
                pe.wait_ge(pT_ready, h * G_HEAD + group_of(QB * b + CH * c + CH - 1, GROUPS[CH * c + CH - 1] - 1) + 1)
                if c == 0:
                    pe.wait_ge(v_ready, h * B + b + 1)
                if isinstance(h, int) and h == 0 and b == 0:
                    pe.wait_ge(zeros_ready, 2 * NC)
                if not (isinstance(u, int) and u == 0):
                    pe.wait_ge(oT_ready, u)
                nk = CH * (c + 1)
                for j in range(nk):
                    q0 = min(max(0, j - CH * c), CH - 2) * P
                    for part in (pT_hi, pT_lo):
                        last = pe.matmul(out_ps[:, q0:W], v_hl[b][:, j, :], part[c][:, j, q0:W],
                                         start=j == 0 and part is pT_hi, stop=j == nk - 1 and part is pT_lo)
                last.then_inc(oT_psum, 1)

            def project_out(h, b, c, before):
                pe.wait_ge(oT_ready, h * (B * NC) + b * NC + c + 1)
                pe.wait_ge(shared_free, before)
                for j in range(CH):
                    last = pe.matmul(shared_ps[:, j * P:(j + 1) * P], oT[c][:, j * P:(j + 1) * P],
                                     wo[:, h, :], start=True, stop=True)
                last.then_inc(wo_psum, 1)

            def slot(h, s, carried, last):
                scores(h, s)
                if s >= LAG:
                    transpose_probs(h, s - LAG)
                elif carried:
                    transpose_probs(h - 1, s - LAG + S)
                if s in PV_SLOT:
                    values(h, *PV_SLOT[s])
                elif carried and s + S in PV_SLOT:
                    values(h - 1, *PV_SLOT[s + S])
                if s in WO_SLOT:
                    project_out(h, *WO_SLOT[s], shared_index(h, s, last))
                elif carried and s + S in WO_SLOT:
                    project_out(h - 1, *WO_SLOT[s + S], shared_index(h, s, last))
                if s in QK_SLOT:
                    nxt, b, half = QK_SLOT[s]
                    if not (nxt and last):
                        project_qk(h + nxt, b, half, shared_index(h, s, last))

            pe.wait_ge(attn_w_loaded, 16 * 5)
            for half in range(2):
                project_qk(0, 0, half, half)
            pe.wait_ge(shared_free, NC)
            for s in range(S):
                slot(0, s, False, False)
            with pe.Fori(1, H - 1) as h:
                for s in range(S):
                    slot(h, s, True, False)
            for s in range(S):
                slot(H - 1, s, True, True)
            for s in range(S, S + 4):
                if s - LAG < S:
                    transpose_probs(H - 1, s - LAG)
                if s in PV_SLOT:
                    values(H - 1, *PV_SLOT[s])
                if s in WO_SLOT:
                    project_out(H - 1, *WO_SLOT[s], H * N_SHARED - 1)

            pe.wait_ge(shared_free, H * N_SHARED)
            transposes(1)
            pe.transpose(shared_ps[:, 0:NE * HB], bfc_rows[:], ident[0:NE * HB, 0:NE * HB]).then_inc(bfc_T_psum, 1)
            pe.wait_ge(wr_ready, 1)
            for t in range(NB):
                if t % CH == 0:
                    pe.wait_ge(nT_ready, NCH + t // CH + 1)
                rows = slice(t * P, (t + 1) * P)
                last = three(out_ps[:, t * E:(t + 1) * E], nT_hi[:, rows], nT_lo[:, rows], wr_hi[:], wr_lo[:])
            last.then_inc(logit_psum, 1)

            def hidden_units(e, c, i):
                for k in range(HB):
                    if not (isinstance(e, int) and e == 0 and c == 0):
                        pe.wait_ge(hidden_ready, e * (NCH * HB) + (c - 1) * HB + k + 1)
                    ws, ts = slice(k * P, (k + 1) * P), slice(c * W, (c + 1) * W)
                    three(banks[k], wfc_hi[i][:, ws], wfc_lo[i][:, ws], nT_hi[:, ts], nT_lo[:, ts])\
                        .then_inc(fc_psum, 1)

            def second_layer(e, c, i):
                pe.wait_ge(hidden_ready, e * (NCH * HB) + c * HB + HB)
                if not (isinstance(e, int) and e == 0 and c < 2):
                    pe.wait_ge(moe_added, e * NCH + c - 1)
                for j in range(CH):
                    for k in range(HB):
                        o = (k % 2) * W + j * P
                        last = pe.matmul(trans_ps[c % 2][:, j * P:(j + 1) * P], hidden[c % 2][k // 2][:, o:o + P],
                                         wproj[i][:, k, :], start=k == 0, stop=k == HB - 1)
                last.then_inc(moe_psum, 1)

            def expert(e, i, before):
                pe.wait_ge(wfc_ready, e + 1)
                for c in range(NCH):
                    hidden_units(e, c, i)
                    if c:
                        second_layer(e, c - 1, i)
                    else:
                        second_layer(before, NCH - 1, 1 - i)

            def gated_biases():
                pe.wait_ge(gate_ready, 1)
                for c in range(NCH):
                    if c:
                        pe.wait_ge(gate_T_ready, 2 * c)
                    for j in range(CH):
                        last = pe.transpose(out_ps[0:NE, j * P:(j + 1) * P], gate[:, CH * c + j, :], ident[:])
                    last.then_inc(gate_T_psum, 1)
                    pe.wait_ge(gate_T_ready, 2 * c + 1)
                    if c == 0:
                        pe.wait_ge(bfc_ready, 1)
                    for j in range(CH):
                        o = c * W + j * P
                        last = pe.matmul(shared_ps[:, j * P:(j + 1) * P], gate_T[:, o:o + P], bproj_rows[:],
                                         start=True, stop=True)
                    last.then_inc(bias_psum, 1)

            pe.wait_ge(wfc_ready, 1)
            hidden_units(0, 0, 0)
            hidden_units(0, 1, 0)
            second_layer(0, 0, 0)
            gated_biases()
            for c in range(2, NCH):
                hidden_units(0, c, 0)
                second_layer(0, c - 1, 0)
            with pe.Fori(1, NE - 1, 2) as e:
                expert(e, 1, e - 1)
                expert(e + 1, 0, e)
            second_layer(NE - 1, NCH - 1, 0)


_INS = ["L0_attn_x", "L0_attn_Wq", "L0_attn_Wk", "L0_attn_Wv", "L0_attn_Wo", "L0_attn_bo",
        "L0_attn_rel_pos_bias", "L0_ffn_Wfc_s", "L0_ffn_bfc_s", "L0_ffn_Wproj_s", "L0_ffn_bproj_s",
        "L0_ffn_Wr", "L0_ffn_Wfc", "L0_ffn_bfc", "L0_ffn_Wproj", "L0_ffn_bproj"]


def kernel(**inputs):
    import numpy as _np
    import concourse.bacc as _bacc
    from concourse import mybir as _mybir
    from concourse.bass_utils import run_bass_kernel_spmd as _run

    nc = _bacc.Bacc("TRN2", target_bir_lowering=False, num_devices=1)
    arrays, args = {}, []
    for name in _INS:
        a = _np.ascontiguousarray(inputs[name])
        arrays[f"in_{name}"] = a
        args.append(nc.dram_tensor(f"in_{name}", a.shape, _mybir.dt.from_np(a.dtype), kind="ExternalInput").ap())
    shape = inputs["L0_attn_x"].shape
    args.append(nc.dram_tensor("out_0", shape, _mybir.dt.float32, kind="ExternalOutput").ap())
    transformer_block(nc, *args)
    r = _run(nc, [arrays], core_ids=[0])
    return r.results[0]["out_0"]
```

```python
from contextlib import ExitStack

import concourse.bass as bass
from concourse import mybir


def transformer_block(
    nc: bass.Bass,
    x: bass.AP,
    Wq: bass.AP,
    Wk: bass.AP,
    Wv: bass.AP,
    Wo: bass.AP,
    bo: bass.AP,
    rel_pos_bias: bass.AP,
    Wfc_s: bass.AP,
    bfc_s: bass.AP,
    Wproj_s: bass.AP,
    bproj_s: bass.AP,
    Wr: bass.AP,
    Wfc: bass.AP,
    bfc: bass.AP,
    Wproj: bass.AP,
    bproj: bass.AP,
    out: bass.AP,
):
    f32 = mybir.dt.float32
    f32r = mybir.dt.float32r
    ALU = mybir.AluOpType
    ACT = mybir.ActivationFunctionType
    AX = mybir.AxisListType.X

    P = 128
    B, T, D = x.shape
    H, R = rel_pos_bias.shape
    HD = Wq.shape[1]
    DH = HD // H
    NB = B * T // P
    QB = T // P
    S = B * QB
    CH = 4
    W = CH * P
    NC = QB // CH
    E = Wr.shape[1]
    NE = E + 1
    HID = Wfc_s.shape[1]
    HB = HID // P
    NCH = NB // CH
    EPS = 1e-5
    MASKED = 1e30
    SCALE = -1.0 / DH
    assert (P, D, R, DH, B, NC) == (128, 128, 128, 64, 2, 2)

    LAG_PE = 2
    LAG_ACT = 2
    LAG_DVE = 2
    GROUPS = [1 if i < CH else 2 for i in range(QB)]
    G_UNIT = sum(GROUPS)
    G_HEAD = B * G_UNIT

    def group_of(s, g):
        return (s // QB) * G_UNIT + sum(GROUPS[: s % QB]) + g

    PV_SLOT = {}
    WO_SLOT = {}
    PV0 = [7, 8, 9, 9]
    PV1 = [10, 11, 12, 12, 12, 13, 13, 13]
    WO = [11, 15]
    QK = [0, 1]
    for _b in range(B):
        for _c, _pv in enumerate((PV0, PV1)):
            for _s in sorted(set(_pv)):
                PV_SLOT[QB * _b + _s] = (_b, _c, _pv.index(_s), len(_pv) - _pv[::-1].index(_s))
            WO_SLOT[QB * _b + WO[_c]] = (_b, _c)
    QK_SLOT = {QK[0]: (0, 1, 0), QK[1]: (0, 1, 1), QB + QK[0]: (1, 0, 0), QB + QK[1]: (1, 0, 1)}
    TAIL = max(WO_SLOT) + 1
    NORM_SLOT = max(WO_SLOT) - CH - 1
    NORMS = ([(0, c) for c in range(NCH)] + [(1, 0), (2, 0), (1, 1), (2, 1)]
             + [(n, c) for n in (1, 2) for c in range(NC, NCH)] + [(3, c) for c in range(NCH)])
    norms_to = lambda n, c: NORMS.index((n, c)) + 1
    SHARED_USE = sorted([(s, "qk", n, b, half) for s, (n, b, half) in QK_SLOT.items()]
                        + [(s % S, "wo", -(s // S), b, c) for s, (b, c) in WO_SLOT.items()])

    assert len({u[0] for u in SHARED_USE}) == len(SHARED_USE)
    N_TURN = H * 2 * P // W

    v_dram = nc.dram_tensor("v_scratch", (B * T, HD), f32, kind="Internal").ap()
    bias_dram = nc.dram_tensor("bias_scratch", (H, 3 * P), f32, kind="Internal").ap()

    ctx = ExitStack()
    with ctx:
        def sb(name, shape, dt=f32):
            return ctx.enter_context(nc.sbuf_tensor(name, shape, dt))

        def pb(name, shape):
            return ctx.enter_context(nc.psum_tensor(name, shape, f32))

        def sem(name):
            return ctx.enter_context(nc.semaphore(name))

        x_sb = sb("x_sb", [P, NB, D])
        normed = sb("normed", [P, NB, D])
        acc = sb("acc", [P, NB, D])
        nT_hi = sb("nT_hi", [P, B * T], f32r)
        nT_lo = sb("nT_lo", [P, B * T], f32r)
        wqk = sb("wqk", [P, H, 2 * DH])
        wqk_hi = sb("wqk_hi", [P, 2 * DH], f32r)
        wqk_lo = sb("wqk_lo", [P, 2 * DH], f32r)
        wv = sb("wv", [P, HD])
        wo = sb("wo", [P, H, D])
        rel = sb("rel", [H, R])
        bias_line = sb("bias_line", [H, 3 * P])
        bias_all = sb("bias_all", [P, H, 2 * P])
        bias_b = [sb(f"bias_{b}", [P, 2 * P]) for b in range(B)]
        q_hl = [sb(f"q_hl{b}", [P, T], f32r) for b in range(B)]
        k_hl = [sb(f"k_hl{b}", [P, 2, T], f32r) for b in range(B)]
        v_raw = [sb(f"v_raw{b}", [P, QB, DH]) for b in range(B)]
        v_hl = [sb(f"v_hl{b}", [P, QB, 2 * DH], f32r) for b in range(B)]
        probs = [sb(f"probs{r}", [P, T]) for r in range(4)]
        pT_hi = [sb(f"pT_hi{c}", [P, CH * (c + 1), W], f32r) for c in range(NC)]
        pT_lo = [sb(f"pT_lo{c}", [P, CH * (c + 1), W], f32r) for c in range(NC)]
        oT = [sb(f"oT{c}", [P, W]) for c in range(NC)]
        head_out = [sb(f"head_out{c}", [P, W]) for c in range(NC)]
        far_min = sb("far_min", [P, S])
        row_min = sb("row_min", [P, S])
        row_sum = sb("row_sum", [P, S])
        row_inv = sb("row_inv", [P, S])
        ident = sb("ident", [P, P])
        exchange = sb("exchange", [P, P])
        stats = sb("stats", [P, NB, 6])
        mv = sb("mv", [P, NB, 2])
        var_eps = sb("var_eps", [P, NB])
        std = sb("std", [P, NB])
        newton = sb("newton", [P, NB])
        rstd = sb("rstd", [P, NB])
        wv_hi = pT_hi[1][:, 0:2, :].rearrange("p a b -> p (a b)")
        wv_lo = pT_lo[1][:, 0:2, :].rearrange("p a b -> p (a b)")
        wfc_raw = [sb(f"wfc_raw{i}", [P, HID]) for i in range(2)]
        wfc_hi = [pT_hi[0][:, i, :] for i in range(2)]
        wfc_lo = [pT_lo[0][:, i, :] for i in range(2)]
        wproj = [sb(f"wproj{i}", [P, HB, D]) for i in range(2)]
        bfc_rows = sb("bfc_rows", [NE * HB, P])
        bfc_cols = sb("bfc_cols", [P, NE * HB])
        hidden = [[probs[2 * i + j] for j in range(2)] for i in range(2)]
        wr = sb("wr", [P, E])
        wr_hi = sb("wr_hi", [P, E], f32r)
        wr_lo = sb("wr_lo", [P, E], f32r)
        bproj_blocks = sb("bproj_blocks", [CH * NE, W])
        logit = sb("logit", [P, NB, E])
        rank = sb("rank", [P, NB, E])
        pick = [sb(f"pick{i}", [P, NB, E]) for i in range(2)]
        order = sb("order", [P, E])
        top = [sb(f"top{i}", [P, NB]) for i in range(2)]
        first = sb("first", [P, NB])
        gate = sb("gate", [P, NB, NE])
        gate_T = wqk[0:CH * NE, 0:CH, :]
        shift = sb("shift", [P, NB])

        score_ps = pb("score_ps", [P, 2 * T])
        trans_ps = [pb(f"trans_ps{r}", [P, W]) for r in range(2)]
        out_ps = pb("out_ps", [P, W])
        shared_ps = pb("shared_ps", [P, W])
        banks = [score_ps[:, r * W:(r + 1) * W] for r in range(4)]

        def scores_of(i):
            return score_ps[:, i * W:(i + 1) * W] if i < CH else score_ps[:, (i % 2) * T:(i % 2 + 1) * T]

        def scores_before(i):
            banks_of = lambda j: {j} if j < CH else {2 * (j % 2), 2 * (j % 2) + 1}
            return max(j for j in range(i - QB, i) if banks_of(j % QB) & banks_of(i)) + 1

        act_passed = sem("act_passed")
        dve_passed = sem("dve_passed")
        pool_passed = sem("pool_passed")
        x_loaded = [sem(f"x_loaded{c}") for c in range(NCH)]
        wqk_loaded = sem("wqk_loaded")
        wv_loaded = sem("wv_loaded")
        wo_loaded = sem("wo_loaded")
        rel_loaded = sem("rel_loaded")
        small_loaded = sem("small_loaded")
        blocks_zeroed = sem("blocks_zeroed")
        bias_line_stored = sem("bias_line_stored")
        bias_loaded = sem("bias_loaded")
        bias_turn_psum = sem("bias_turn_psum")
        bias_turned = sem("bias_turned")
        ident_ready = sem("ident_ready")
        pool_done = sem("pool_done")
        dve_done = sem("dve_done")
        wqk_scaled = sem("wqk_scaled")
        wv_hi_done = sem("wv_hi_done")
        wv_split = sem("wv_split")
        var_ready = sem("var_ready")
        std_ready = sem("std_ready")
        normed_ready = sem("normed_ready")
        nT_psum = sem("nT_psum")
        nT_hi_ready = sem("nT_hi_ready")
        nT_ready = sem("nT_ready")
        v_psum = sem("v_psum")
        v_evac_act = sem("v_evac_act")
        v_evac_dve = sem("v_evac_dve")
        v_stored = [sem(f"v_stored{r}") for r in range(4)]
        zeros_ready = sem("zeros_ready")
        wqk_hi_done = sem("wqk_hi_done")
        wqk_ready = sem("wqk_ready")
        bias_ready = sem("bias_ready")
        v_loaded = [sem(f"v_loaded{b}") for b in range(B)]
        v_hi_done = sem("v_hi_done")
        v_ready = sem("v_ready")
        qk_psum = sem("qk_psum")
        qk_hi = sem("qk_hi")
        qk_lo = sem("qk_lo")
        q_copied = [sem(f"q_copied{b}") for b in range(B)]
        acc_started = sem("acc_started")
        acc_added = sem("acc_added")
        k_copied = [sem(f"k_copied{b}") for b in range(B)]
        scores_ready = sem("scores_ready")
        far_ready = sem("far_ready")
        min_ready = sem("min_ready")
        probs_ready = sem("probs_ready")
        pT_psum = sem("pT_psum")
        pT_hi_ready = sem("pT_hi_ready")
        pT_ready = sem("pT_ready")
        inv_ready = sem("inv_ready")
        oT_psum = sem("oT_psum")
        oT_ready = sem("oT_ready")
        wo_psum = sem("wo_psum")
        wo_scaled = sem("wo_scaled")
        moe_w_loaded = [sem(f"moe_w_loaded{i}") for i in range(2)]
        wfc_hi_done = sem("wfc_hi_done")
        wfc_ready = sem("wfc_ready")
        wr_ready = sem("wr_ready")
        logit_psum = sem("logit_psum")
        exp_ready = sem("exp_ready")
        logit_ready = sem("logit_ready")
        gate_ready = sem("gate_ready")
        gate_T_psum = sem("gate_T_psum")
        gate_T_ready = sem("gate_T_ready")
        bias_added = sem("bias_added")
        bias_psum = sem("bias_psum")
        bfc_T_psum = sem("bfc_T_psum")
        bfc_ready = sem("bfc_ready")
        fc_psum = sem("fc_psum")
        hidden_ready = sem("hidden_ready")
        moe_psum = sem("moe_psum")
        moe_added = sem("moe_added")
        result_ready = sem("result_ready")
        result_stored = sem("result_stored")

        block = ctx.enter_context(nc.Block())
        x_blocks = x.rearrange("b (t p) d -> p (b t) d", p=P)
        out_blocks = out.rearrange("b (t p) d -> p (b t) d", p=P)

        @block.sync
        def _(sp):
            for c in range(NCH):
                sp.dma_start(x_sb[:, CH * c:CH * (c + 1), :],
                             x_blocks[:, CH * c:CH * (c + 1), :]).then_inc(x_loaded[c], 16)

            sp.wait_ge(dve_done, 2)
            sp.dma_start(bias_dram, bias_line[:]).then_inc(bias_line_stored, 16)
            sp.wait_ge(bias_line_stored, 16)
            sp.dma_start(bias_all[:], bass.AP(bias_dram.tensor, 0, [[1, P], [3 * P, H], [1, 2 * P]]))\
              .then_inc(bias_loaded, 16)

            for r in range(2):
                sp.dma_start(wo[r * DH:(r + 1) * DH, :, :],
                             Wo.rearrange("(h d) n -> d h n", h=H)).then_inc(wo_loaded, 16)

            def store_v(t):
                sp.wait_ge(v_evac_act, t + 1)
                sp.wait_ge(v_evac_dve, t + 1)
                sp.dma_start(v_dram[t * P:(t + 1) * P, :], probs[t % 4][:]).then_inc(v_stored[t % 4], 16)

            def load_v(h, b):
                src = bass.AP(v_dram.tensor, h * DH + b * T * HD, [[HD, P], [P * HD, QB], [1, DH]])
                sp.dma_start(v_raw[b][:], src).then_inc(v_loaded[b], 16)

            def place_qk(h, b):
                sp.wait_ge(qk_lo, h * (2 * B) + 2 * b + 2)
                for part in range(2):
                    sp.dma_start(q_hl[b][part * DH:(part + 1) * DH, :].bitcast(f32),
                                 k_hl[b][0:DH, part, :].bitcast(f32)).then_inc(q_copied[b], 16)
                sp.wait_ge(q_copied[b], h * 32 + 32)
                sp.dma_start(k_hl[b][0:DH, :, :].bitcast(f32), k_hl[b][DH:P, :, :].bitcast(f32))\
                  .then_inc(k_copied[b], 16)

            def head(h, last=False):
                if not (isinstance(h, int) and h == 0):
                    sp.wait_ge(v_ready, h * B)
                load_v(h, 1)
                place_qk(h, 1)
                if not last:
                    sp.wait_ge(v_ready, h * B + 1)
                    load_v(h + 1, 0)
                    place_qk(h + 1, 0)

            place_qk(0, 0)
            for t in range(NB):
                store_v(t)
            for r in range(4):
                sp.wait_ge(v_stored[r], 16 * (NB // 4))
            load_v(0, 0)
            head(0)
            with sp.Fori(1, H - 1) as h:
                head(h)
            head(H - 1, last=True)

            def load_expert(i, wf, wp):
                sp.dma_start(wfc_raw[i][:], wf).then_inc(moe_w_loaded[i], 16)
                sp.dma_start(wproj[i][:], wp).then_inc(moe_w_loaded[i], 16)

            load_expert(0, Wfc_s, Wproj_s.rearrange("(k p) n -> p k n", p=P))
            load_expert(1, Wfc[0, :, :], Wproj[0, :, :].rearrange("(k p) n -> p k n", p=P))

            def expert_src(e):
                return (bass.AP(Wfc.tensor, (e - 1) * (D * HID), [[HID, P], [1, HID]]),
                        bass.AP(Wproj.tensor, (e - 1) * (D * HID), [[D, P], [P * D, HB], [1, D]]))

            def reload(e, i):
                sp.wait_ge(moe_psum, (e - 1) * NCH)
                load_expert(i, *expert_src(e))

            with sp.Fori(2, NE - 1, 2) as e:
                reload(e, 0)
                reload(e + 1, 1)
            reload(NE - 1, 0)

            for c in range(NCH):
                sp.wait_ge(result_ready, c + 1)
                sp.dma_start(out_blocks[:, CH * c:CH * (c + 1), :],
                             normed[:, CH * c:CH * (c + 1), :]).then_inc(result_stored, 16)
            sp.wait_ge(result_stored, 16 * NCH)

        @block.gpsimd
        def _(pool):
            own = [0]

            def then_wait(ins):
                own[0] += 1
                ins.then_inc(pool_done, 1)
                pool.wait_ge(pool_done, own[0])

            then_wait(pool.memset(ident[:], 0.0))
            pool.affine_select(out=ident[:], in_=ident[:], compare_op=ALU.not_equal, fill=1.0, base=0,
                               pattern=[[-1, P]], channel_multiplier=1).then_inc(ident_ready, 1)
            then_wait(pool.memset(exchange[:], 0.0))
            pool.affine_select(out=exchange[:], in_=exchange[:], compare_op=ALU.not_equal, fill=1.0,
                               base=1 - P, pattern=[[1, P]], channel_multiplier=1).then_inc(ident_ready, 1)

            def split_wqk(h):
                pool.sem_inc(pool_passed, 1)
                pool.tensor_copy(wqk_hi[:], wqk[:, h, :]).then_inc(wqk_hi_done, 1)
                pool.wait_ge(wqk_hi_done, h + 1)
                pool.sem_inc(pool_passed, 1)
                pool.tensor_tensor(wqk_lo[:], wqk[:, h, :], wqk_hi[:], ALU.subtract).then_inc(wqk_ready, 1)

            def take_bias(h, b):
                pool.sem_inc(pool_passed, 1)
                pool.tensor_copy(bias_b[b][:], bias_all[:, h, :]).then_inc(bias_ready, 1)

            def zero_pads():
                for c in range(NC):
                    for part in (pT_hi, pT_lo):
                        zero = part[c][:, CH * c + CH - 1, (CH - 2) * P:(CH - 1) * P]
                        pool.tensor_scalar(zero, ident[:], 0.0, None, ALU.mult).then_inc(zeros_ready, 1)

            def split_v(h, b):
                n = h * B + b
                pool.wait_ge(v_loaded[b], h * 16 + 16)
                pool.sem_inc(pool_passed, 1)
                pool.tensor_copy(v_hl[b][:, :, 0:DH], v_raw[b][:]).then_inc(v_hi_done, 1)
                pool.wait_ge(v_hi_done, n + 1)
                pool.tensor_tensor(v_hl[b][:, :, DH:2 * DH], v_raw[b][:], v_hl[b][:, :, 0:DH],
                                   ALU.subtract).then_inc(v_ready, 1)

            def add_head(h, b, c):
                n = h * (B * NC) + b * NC + c
                pool.wait_ge(wo_scaled, n + 1)
                if not (isinstance(n, int) and n == 0):
                    pool.wait_ge(acc_added, n)
                blocks = slice(QB * b + CH * c, QB * b + CH * (c + 1))
                pool.tensor_tensor(acc[:, blocks, :], acc[:, blocks, :],
                                   head_out[c][:].rearrange("p (t d) -> p t d", d=D), ALU.add)\
                    .then_inc(acc_added, 1)

            def slot(h, s, carried, last):
                if carried and s + S in WO_SLOT:
                    add_head(h - 1, *WO_SLOT[s + S])
                if s in WO_SLOT:
                    add_head(h, *WO_SLOT[s])
                if s == 1:
                    if carried:
                        pool.wait_ge(min_ready, h * S)
                    take_bias(h, 1)
                if s == 5:
                    pool.wait_ge(qk_psum, h * (2 * B) + 2 * B)
                    if not last:
                        split_wqk(h + 1)
                    if carried:
                        pool.wait_ge(oT_psum, h * (B * NC))
                    split_v(h, 1)
                if s == QB and not last:
                    pool.wait_ge(min_ready, h * S + QB)
                    take_bias(h + 1, 0)
                if s == QB + 5 and not last:
                    pool.wait_ge(oT_psum, h * (B * NC) + NC)
                    split_v(h + 1, 0)

            pool.wait_ge(wqk_loaded, 32)
            pool.wait_ge(wqk_scaled, 1)
            split_wqk(0)
            pool.wait_ge(wv_hi_done, 1)
            pool.tensor_tensor(wv_lo, wv[:], wv_hi, ALU.subtract).then_inc(wv_split, 1)
            zero_pads()

            pool.dma_start(acc[:], bass.AP(bo.tensor, 0, [[0, P], [0, NB], [1, D]])).then_inc(acc_started, 16)
            pool.dma_start(wr[:], Wr).then_inc(small_loaded, 16)
            pool.dma_start(bfc_rows[0:HB, :], bfc_s.rearrange("(k p) -> k p", p=P)).then_inc(small_loaded, 16)
            pool.dma_start(bfc_rows[HB:NE * HB, :], bfc.rearrange("e (k p) -> (e k) p", p=P)).then_inc(small_loaded, 16)
            pool.memset(bproj_blocks[:], 0.0).then_inc(blocks_zeroed, 1)
            pool.wait_ge(blocks_zeroed, 1)
            for j in range(CH):
                row, cols = j * NE, slice(j * D, (j + 1) * D)
                pool.dma_start(bproj_blocks[row:row + 1, cols],
                               bproj_s.rearrange("(a n) -> a n", a=1)).then_inc(small_loaded, 16)
                pool.dma_start(bproj_blocks[row + 1:row + NE, cols], bproj).then_inc(small_loaded, 16)

            pool.wait_ge(bias_turned, N_TURN)
            take_bias(0, 0)
            pool.wait_ge(acc_started, 16)
            split_v(0, 0)
            for s in range(S):
                slot(0, s, False, False)
            with pool.Fori(1, H - 1) as h:
                for s in range(S):
                    slot(h, s, True, False)
            for s in range(S):
                slot(H - 1, s, True, True)
            def split_wfc(e, i):
                pool.wait_ge(moe_w_loaded[i], (e - i) * 16 + 32)
                pool.sem_inc(pool_passed, 1)
                pool.tensor_copy(wfc_hi[i], wfc_raw[i][:]).then_inc(wfc_hi_done, 1)
                pool.wait_ge(wfc_hi_done, e + 1)
                pool.tensor_tensor(wfc_lo[i], wfc_raw[i][:], wfc_hi[i], ALU.subtract).then_inc(wfc_ready, 1)

            pool.wait_ge(small_loaded, 16 * (3 + 2 * CH))
            then_wait(pool.tensor_copy(wr_hi[:], wr[:]))
            pool.tensor_tensor(wr_lo[:], wr[:], wr_hi[:], ALU.subtract).then_inc(wr_ready, 1)
            for s in range(S, TAIL):
                if s in WO_SLOT:
                    if WO_SLOT[s] == (B - 1, NC - 1):
                        pool.wait_ge(oT_psum, H * B * NC - 1)
                        split_wfc(0, 0)
                    add_head(H - 1, *WO_SLOT[s])
            split_wfc(1, 1)

            def resplit(e, i):
                pool.wait_ge(fc_psum, (e - 1) * (NCH * HB))
                split_wfc(e, i)

            with pool.Fori(2, NE - 1, 2) as e:
                resplit(e, 0)
                resplit(e + 1, 1)
            resplit(NE - 1, 0)

        @block.scalar
        def _(act):
            act.dma_start(rel[:], rel_pos_bias).then_inc(rel_loaded, 16)
            act.dma_start(wqk[:, :, 0:DH], Wq.rearrange("p (h d) -> p h d", h=H)).then_inc(wqk_loaded, 16)
            act.dma_start(wqk[:, :, DH:2 * DH], Wk.rearrange("p (h d) -> p h d", h=H)).then_inc(wqk_loaded, 16)
            act.dma_start(wv[:], Wv).then_inc(wv_loaded, 16)

            def root(n, c):
                act.wait_ge(var_ready, norms_to(n, c))
                act.activation(std[:, CH * c:CH * (c + 1)], var_eps[:, CH * c:CH * (c + 1)], ACT.Sqrt)\
                   .then_inc(std_ready, 1)

            def nT_evac(n, c):
                act.wait_ge(nT_psum, n * NCH + c + 1)
                act.activation(nT_hi[:, c * W:(c + 1) * W], trans_ps[c % 2][:], ACT.Copy)\
                   .then_inc(nT_hi_ready, 1)

            def split_qk_hi(h, b, half):
                act.wait_ge(qk_psum, h * (2 * B) + 2 * b + half + 1)
                if not (isinstance(h, int) and h == 0):
                    act.wait_ge(scores_ready, h * S + QB * b + QB - S)
                act.activation(k_hl[b][:, 0, half * W:(half + 1) * W], shared_ps[:], ACT.Copy).then_inc(qk_hi, 1)

            root(0, 0)
            root(0, 1)
            act.wait_ge(wqk_loaded, 32)
            act.activation(wqk[:, :, 0:DH], wqk[:, :, 0:DH], ACT.Copy, scale=SCALE).then_inc(wqk_scaled, 1)
            root(0, 2)
            root(0, 3)
            act.wait_ge(wv_loaded, 16)
            act.activation(wv_hi, wv[:], ACT.Copy).then_inc(wv_hi_done, 1)
            nT_evac(0, 0)
            nT_evac(0, 1)
            split_qk_hi(0, 0, 0)
            nT_evac(0, 2)
            split_qk_hi(0, 0, 1)
            nT_evac(0, 3)

            bias_flat = bias_all[:].rearrange("p h c -> p (h c)")
            for t in range(NB):
                act.wait_ge(v_psum, 2 * t + 1)
                if t >= 4:
                    act.wait_ge(v_stored[t % 4], 16 * (t // 4))
                act.activation(probs[t % 4][:, 0:W], banks[(2 * t) % 4], ACT.Copy).then_inc(v_evac_act, 1)
                n = t - (NB - N_TURN)
                if n >= 0:
                    act.wait_ge(bias_turn_psum, n + 1)
                    act.activation(bias_flat[:, n * W:(n + 1) * W], trans_ps[n % 2][:], ACT.Copy)\
                       .then_inc(bias_turned, 1)
            for r in range(4):
                act.wait_ge(v_stored[r], 16 * (NB // 4))

            def exp(h, s):
                n = P * (s % QB + 1)
                act.wait_ge(min_ready, h * S + s + 1)
                act.activation(probs[s % 4][:, 0:n], scores_of(s % QB)[:, 0:n], ACT.Exp,
                               bias=row_min[:, s:s + 1], scale=-1.0,
                               accum_out=row_sum[:, s:s + 1]).then_inc(probs_ready, 1)

            def split_hi(h, s):
                b, i = divmod(s, QB)
                c, q = divmod(i, CH)
                u = h * (B * NC) + b * NC + c
                if q == 0 and not (isinstance(u, int) and u < NC):
                    act.wait_ge(oT_psum, u - (NC - 1))
                for g in range(GROUPS[i]):
                    k = group_of(s, g)
                    m = min(CH, i + 1 - CH * g)
                    act.wait_ge(pT_psum, h * G_HEAD + k + 1)
                    act.activation(pT_hi[c][:, CH * g:CH * g + m, q * P:(q + 1) * P],
                                   trans_ps[k % 2][:, 0:m * P].rearrange("p (m q) -> p m q", q=P),
                                   ACT.Copy).then_inc(pT_hi_ready, 1)

            def copy_oT(h, b, c, j0, j1):
                if j1 < CH * (c + 1):
                    return
                act.wait_ge(oT_psum, h * (B * NC) + b * NC + c + 1)
                act.activation(oT[c][:], out_ps[:], ACT.Copy).then_inc(oT_ready, 1)

            def slot(h, s, carried, last):
                if s >= LAG_ACT:
                    split_hi(h, s - LAG_ACT)
                elif carried:
                    split_hi(h - 1, s - LAG_ACT + S)
                exp(h, s)
                if s in PV_SLOT:
                    copy_oT(h, *PV_SLOT[s])
                if carried and s + S in PV_SLOT:
                    copy_oT(h - 1, *PV_SLOT[s + S])
                if s in QK_SLOT:
                    nxt, b, half = QK_SLOT[s]
                    if not (nxt and last):
                        split_qk_hi(h + nxt, b, half)

            for s in range(S):
                slot(0, s, False, False)
            with act.Fori(1, H - 1) as h:
                for s in range(S):
                    slot(h, s, True, False)
            for s in range(S):
                slot(H - 1, s, True, True)
            for s in range(S, TAIL):
                if s - LAG_ACT < S:
                    split_hi(H - 1, s - LAG_ACT)
                if s in PV_SLOT:
                    copy_oT(H - 1, *PV_SLOT[s])
                if s == NORM_SLOT:
                    root(1, 0)
                    root(2, 0)
            root(1, 1)
            root(2, 1)
            for c in range(NC):
                nT_evac(1, c)
            for n in (1, 2):
                for c in range(NC, NCH):
                    root(n, c)

            def gelu(e, c, i):
                for k in range(HB):
                    act.wait_ge(fc_psum, e * (NCH * HB) + c * HB + k + 1)
                    if k == 0 and not (isinstance(e, int) and e == 0 and c < 2):
                        act.wait_ge(moe_psum, e * NCH + c - 1)
                    act.sem_inc(act_passed, 1)
                    act.activation(hidden[c % 2][k // 2][:, (k % 2) * W:(k % 2 + 1) * W], banks[k],
                                   ACT.Gelu_apprx_tanh, bias=bfc_cols[:, bass.ds(e * HB + k, 1)]).then_inc(hidden_ready, 1)

            act.wait_ge(bfc_T_psum, 1)
            act.activation(bfc_cols[:], shared_ps[:, 0:NE * HB], ACT.Copy).then_inc(bfc_ready, 1)
            act.wait_ge(bfc_ready, 1)
            gelu(0, 0, 0)
            gelu(0, 1, 0)
            for c in range(NC, NCH):
                nT_evac(1, c)
            act.wait_ge(logit_ready, 1)
            act.activation(rank[:], logit[:], ACT.Exp).then_inc(exp_ready, 1)
            gelu(0, 2, 0)
            gelu(0, 3, 0)
            with act.Fori(1, NE - 1, 2) as e:
                for c in range(NCH):
                    gelu(e, c, 1)
                for c in range(NCH):
                    gelu(e + 1, c, 0)

            for c in range(NCH):
                root(3, c)

        @block.vector
        def _(dve):
            own = [0]

            def then_wait(ins):
                own[0] += 1
                ins.then_inc(dve_done, 1)
                dve.wait_ge(dve_done, own[0])

            dve.memset(bias_line[:, 0:P], 0.0)
            then_wait(dve.memset(bias_line[:, 2 * P:3 * P], MASKED))
            dve.wait_ge(rel_loaded, 16)
            then_wait(dve.tensor_scalar(bias_line[:, P:2 * P], rel[:], rel[:, 0:1], SCALE,
                                        ALU.subtract, ALU.mult))

            def moments(src, c):
                lo, hi = CH * c, CH * (c + 1)
                for t in range(lo, hi):
                    last = dve.bn_stats(stats[:, t, :], src[:, t, :])
                then_wait(last)
                for t in range(lo, hi):
                    last = dve.bn_aggr(mv[:, t, :], stats[:, t, :])
                then_wait(last)
                dve.tensor_scalar(var_eps[:, lo:hi], mv[:, lo:hi, 1], EPS, None, ALU.add).then_inc(var_ready, 1)

            def inverse_std(n, c):
                lo, hi = CH * c, CH * (c + 1)
                r, v, t = rstd[:, lo:hi], var_eps[:, lo:hi], newton[:, lo:hi]
                dve.wait_ge(std_ready, norms_to(n, c))
                then_wait(dve.reciprocal(r, std[:, lo:hi]))
                then_wait(dve.tensor_tensor(t, r, r, ALU.mult))
                then_wait(dve.tensor_tensor(t, t, v, ALU.mult))
                then_wait(dve.tensor_scalar(t, t, -0.5, 1.5, ALU.mult, ALU.add))
                then_wait(dve.tensor_tensor(r, r, t, ALU.mult))

            def normalise(dst, src, c):
                for t in range(CH * c, CH * (c + 1)):
                    last = dve.tensor_scalar(dst[:, t, :], src[:, t, :], mv[:, t, 0:1], rstd[:, t:t + 1],
                                             ALU.subtract, ALU.mult)
                return last

            def nT_evac(n, c):
                dve.wait_ge(nT_hi_ready, n * NCH + c + 1)
                dve.tensor_tensor(nT_lo[:, c * W:(c + 1) * W], trans_ps[c % 2][:],
                                  nT_hi[:, c * W:(c + 1) * W], ALU.subtract).then_inc(nT_ready, 1)

            def split_qk_lo(h, b, half):
                cols = slice(half * W, (half + 1) * W)
                dve.wait_ge(qk_hi, h * (2 * B) + 2 * b + half + 1)
                dve.tensor_tensor(k_hl[b][:, 1, cols], shared_ps[:], k_hl[b][:, 0, cols],
                                  ALU.subtract).then_inc(qk_lo, 1)

            for c in range(NCH):
                dve.wait_ge(x_loaded[c], 16)
                moments(x_sb, c)
            for c in range(NCH):
                inverse_std(0, c)
                normalise(normed, x_sb, c).then_inc(normed_ready, 1)
                if c:
                    nT_evac(0, c - 1)
                if c >= 2:
                    split_qk_lo(0, 0, c - 2)
            nT_evac(0, NCH - 1)
            for t in range(NB):
                dve.wait_ge(v_psum, 2 * t + 2)
                if t >= 4:
                    dve.wait_ge(v_stored[t % 4], 16 * (t // 4))
                dve.tensor_copy(probs[t % 4][:, W:2 * W], banks[(2 * t + 1) % 4]).then_inc(v_evac_dve, 1)

            def row_minimum(h, s):
                b, i = divmod(s, QB)
                ps = scores_of(i)
                n, near = P * (i + 1), min(2 * P, P * (i + 1))
                dve.wait_ge(scores_ready, h * S + s + 1)
                if i == 0:
                    dve.wait_ge(bias_ready, h * B + b + 1)
                start = 3e38
                if i >= 2:
                    dve.tensor_reduce(far_min[:, s:s + 1], ps[:, 0:n - near], AX, ALU.min)\
                       .then_inc(far_ready, 1)
                    dve.wait_ge(far_ready, h * (B * (QB - 2)) + b * (QB - 2) + i - 1)
                    start = far_min[:, s:s + 1]
                dve.sem_inc(dve_passed, 1)
                dve.tensor_tensor_reduce(out=ps[:, n - near:n], in0=ps[:, n - near:n],
                                         in1=bias_b[b][:, 2 * P - near:2 * P], scale=1.0, scalar=start,
                                         op0=ALU.add, op1=ALU.min,
                                         accum_out=row_min[:, s:s + 1]).then_inc(min_ready, 1)

            def split_lo(h, s):
                b, i = divmod(s, QB)
                c, q = divmod(i, CH)
                for g in range(GROUPS[i]):
                    k = group_of(s, g)
                    m = min(CH, i + 1 - CH * g)
                    dst = (slice(None), slice(CH * g, CH * g + m), slice(q * P, (q + 1) * P))
                    dve.wait_ge(pT_hi_ready, h * G_HEAD + k + 1)
                    dve.tensor_tensor(pT_lo[c][dst], trans_ps[k % 2][:, 0:m * P].rearrange("p (m q) -> p m q", q=P),
                                      pT_hi[c][dst], ALU.subtract).then_inc(pT_ready, 1)

            def invert_sums(h, b, c, j0, j1):
                if j0 > 0:
                    return
                s = QB * b + CH * c
                dve.wait_ge(probs_ready, h * S + s + CH)
                dve.reciprocal(row_inv[:, s:s + CH], row_sum[:, s:s + CH]).then_inc(inv_ready, 1)

            def scale_head(h, b, c):
                n = h * (B * NC) + b * NC + c
                dve.wait_ge(wo_psum, n + 1)
                dve.wait_ge(inv_ready, n + 1)
                if not (isinstance(n, int) and n < NC):
                    dve.wait_ge(acc_added, n - (NC - 1))
                blocks = slice(QB * b + CH * c, QB * b + CH * (c + 1))
                dve.tensor_tensor(head_out[c][:].rearrange("p (t d) -> p t d", d=D),
                                  shared_ps[:].rearrange("p (t d) -> p t d", d=D),
                                  row_inv[:, blocks].unsqueeze(2).broadcast_to([P, CH, D]),
                                  ALU.mult).then_inc(wo_scaled, 1)

            def slot(h, s, carried, last):
                row_minimum(h, s)
                if s >= LAG_DVE:
                    split_lo(h, s - LAG_DVE)
                elif carried:
                    split_lo(h - 1, s - LAG_DVE + S)
                for slots, do in ((PV_SLOT, invert_sums), (WO_SLOT, scale_head)):
                    if s in slots:
                        do(h, *slots[s])
                    if carried and s + S in slots:
                        do(h - 1, *slots[s + S])
                if s in QK_SLOT:
                    nxt, b, half = QK_SLOT[s]
                    if not (nxt and last):
                        split_qk_lo(h + nxt, b, half)

            for s in range(S):
                slot(0, s, False, False)
            with dve.Fori(1, H - 1) as h:
                for s in range(S):
                    slot(h, s, True, False)
            for s in range(S):
                slot(H - 1, s, True, True)
            def norm_chunks(chunks):
                for c in chunks:
                    moments(acc, c)
                for c in chunks:
                    lo, hi = CH * c, CH * (c + 1)
                    inverse_std(1, c)
                    dve.tensor_tensor(shift[:, lo:hi], mv[:, lo:hi, 0], rstd[:, lo:hi], ALU.mult)
                    for t in range(lo, hi):
                        last = dve.scalar_tensor_tensor(out=x_sb[:, t, :], in0=acc[:, t, :],
                                                        scalar=rstd[:, t:t + 1], in1=x_sb[:, t, :],
                                                        op0=ALU.mult, op1=ALU.add)
                    then_wait(last)
                    moments(x_sb, c)
                for c in chunks:
                    inverse_std(2, c)
                    normalise(normed, x_sb, c).then_inc(normed_ready, 1)

            for s in range(S, TAIL):
                if s - LAG_DVE < S:
                    split_lo(H - 1, s - LAG_DVE)
                if s in PV_SLOT:
                    invert_sums(H - 1, *PV_SLOT[s])
                if s in WO_SLOT:
                    scale_head(H - 1, *WO_SLOT[s])
                if s == NORM_SLOT:
                    dve.wait_ge(acc_added, (H - 1) * B * NC + NC)
                    norm_chunks([0])
            norm_chunks([1])
            for c in range(NC):
                nT_evac(1, c)
            dve.wait_ge(acc_added, H * B * NC)
            norm_chunks(range(NC, NCH))
            for c in range(NC, NCH):
                nT_evac(1, c)

            def add_expert(e, c):
                dve.wait_ge(moe_psum, e * NCH + c + 1)
                if not (isinstance(e, int) and e == 0):
                    dve.wait_ge(moe_added, e * NCH + c - NCH + 1)
                elif c == NCH - 1:
                    dve.wait_ge(bias_added, NCH)
                for j in range(CH):
                    t = CH * c + j
                    product = trans_ps[c % 2][:, j * P:(j + 1) * P]
                    if isinstance(e, int) and e == 0 and c < NCH - 1:
                        last = dve.tensor_copy(acc[:, t, :], product)
                    else:
                        last = dve.scalar_tensor_tensor(out=acc[:, t, :], in0=product,
                                                        scalar=gate[:, t, bass.ds(e, 1)], in1=acc[:, t, :],
                                                        op0=ALU.mult, op1=ALU.add)
                last.then_inc(moe_added, 1)

            def add_biases(c):
                dve.wait_ge(bias_psum, c + 1)
                product = (shared_ps, out_ps)[c % 2][:].rearrange("p (t d) -> p t d", d=D)
                blocks = acc[:, CH * c:CH * (c + 1), :]
                if c < NCH - 1:
                    dve.wait_ge(moe_added, c + 1)
                    dve.tensor_tensor(blocks, blocks, product, ALU.add).then_inc(bias_added, 1)
                else:
                    dve.tensor_copy(blocks, product).then_inc(bias_added, 1)

            add_expert(0, 0)

            for k in range(E):
                last = dve.memset(order[:, k:k + 1], float(E - k))
            then_wait(last)
            dve.wait_ge(logit_psum, 1)
            lps = out_ps[:, 0:NB * E].rearrange("p (t e) -> p t e", e=E)
            each = lambda a: a.unsqueeze(2).broadcast_to([P, NB, E])
            then_wait(dve.tensor_reduce(top[0][:], lps, AX, ALU.max))
            dve.tensor_tensor(logit[:], lps, each(top[0][:]), ALU.subtract).then_inc(logit_ready, 1)
            dve.wait_ge(exp_ready, 1)
            prefer = order[:].unsqueeze(1).broadcast_to([P, NB, E])
            for i in range(2):
                then_wait(dve.tensor_reduce(top[i][:], rank[:], AX, ALU.max))
                then_wait(dve.tensor_tensor(pick[i][:], rank[:], each(top[i][:]), ALU.is_equal))
                then_wait(dve.tensor_tensor(pick[i][:], pick[i][:], prefer, ALU.mult))
                then_wait(dve.tensor_reduce(first[:], pick[i][:], AX, ALU.max))
                then_wait(dve.tensor_tensor(pick[i][:], pick[i][:], each(first[:]), ALU.is_equal))
                if i == 0:
                    then_wait(dve.scalar_tensor_tensor(
                        out=rank[:].rearrange("p t e -> p (t e)"), in0=pick[0][:].rearrange("p t e -> p (t e)"),
                        scalar=-2.0, in1=rank[:].rearrange("p t e -> p (t e)"), op0=ALU.mult, op1=ALU.add))
            then_wait(dve.tensor_tensor(first[:], top[0][:], top[1][:], ALU.add))
            then_wait(dve.reciprocal(first[:], first[:]))
            for i in range(2):
                then_wait(dve.tensor_tensor(top[i][:], top[i][:], first[:], ALU.mult))
                then_wait(dve.tensor_tensor(pick[i][:], pick[i][:], each(top[i][:]), ALU.mult))
            then_wait(dve.memset(gate[:, :, 0:1], 1.0))
            dve.tensor_tensor(gate[:, :, 1:NE], pick[0][:], pick[1][:], ALU.add).then_inc(gate_ready, 1)

            add_expert(0, 1)
            dve.wait_ge(gate_T_psum, 1)
            dve.tensor_copy(gate_T, out_ps[0:CH * NE, :].rearrange("p (c q) -> p c q", q=P))\
               .then_inc(gate_T_ready, 1)
            add_biases(0)
            add_biases(1)
            add_expert(0, 2)
            add_biases(2)
            add_biases(3)
            for t in range(NB):
                dve.tensor_scalar(x_sb[:, t, :], x_sb[:, t, :], shift[:, t:t + 1], None, ALU.subtract)
            add_expert(0, 3)
            dve.wait_ge(bias_added, NCH)
            with dve.Fori(1, NE - 1) as e:
                for c in range(NCH):
                    add_expert(e, c)

            for c in range(NCH):
                add_expert(NE - 1, c)
                dve.wait_ge(moe_added, (NE - 1) * NCH + c + 1)
                moments(acc, c)
                inverse_std(3, c)
                then_wait(normalise(normed, acc, c))
                blocks = slice(CH * c, CH * (c + 1))
                dve.tensor_tensor(normed[:, blocks, :], normed[:, blocks, :], x_sb[:, blocks, :], ALU.add)\
                   .then_inc(result_ready, 1)

        @block.tensor
        def _(pe):
            def three(dst, w_hi, w_lo, m_hi, m_lo, start=True, stop=True):
                pe.matmul(dst, w_hi, m_hi, start=start, stop=False)
                pe.matmul(dst, w_hi, m_lo, start=False, stop=False)
                return pe.matmul(dst, w_lo, m_hi, start=False, stop=stop)

            def transposes(n, c):
                pe.wait_ge(normed_ready, n * NCH + c + 1)
                if n or c >= 2:
                    pe.wait_ge(nT_ready, n * NCH + c - 1)
                for j in range(CH):
                    last = pe.transpose(trans_ps[c % 2][:, j * P:(j + 1) * P], normed[:, CH * c + j, :], ident[:])
                last.then_inc(nT_psum, 1)

            def project_qk(h, b, half):
                pe.wait_ge(wqk_ready, h + 1)
                cols = slice(b * T + half * W, b * T + (half + 1) * W)
                three(shared_ps[:], wqk_hi[:], wqk_lo[:], nT_hi[:, cols], nT_lo[:, cols]).then_inc(qk_psum, 1)

            pe.wait_ge(ident_ready, 1)
            transposes(0, 0)
            transposes(0, 1)
            transposes(0, 2)
            project_qk(0, 0, 0)
            transposes(0, 3)
            pe.wait_ge(qk_lo, 1)
            project_qk(0, 0, 1)

            bias_flat = bias_all[:].rearrange("p h c -> p (h c)")
            pe.wait_ge(wv_split, 1)
            for t in range(NB):
                if t % CH == 0:
                    pe.wait_ge(nT_ready, t // CH + 1)
                for half in range(2):
                    if t >= 2:
                        pe.wait_ge(v_evac_act if half == 0 else v_evac_dve, t - 1)
                    cols, rows = slice(half * W, (half + 1) * W), slice(t * P, (t + 1) * P)
                    three(banks[(2 * t + half) % 4], nT_hi[:, rows], nT_lo[:, rows],
                          wv_hi[:, cols], wv_lo[:, cols]).then_inc(v_psum, 1)
                n = t - (NB - N_TURN)
                if n >= 0:
                    if n == 0:
                        pe.wait_ge(bias_loaded, 16)
                        pe.wait_ge(ident_ready, 2)
                        pe.wait_ge(nT_ready, NCH)
                    if n >= 2:
                        pe.wait_ge(bias_turned, n - 1)
                    pe.matmul(trans_ps[n % 2][:], exchange[:], bias_flat[:, n * W:(n + 1) * W],
                              start=True, stop=True).then_inc(bias_turn_psum, 1)

            def wait_shared(h, s, last):
                uses = [u for u in SHARED_USE if u[0] < s and not (isinstance(h, int) and h == 0 and u[2] < 0)
                        and not (last and u[2] > 0)]
                if isinstance(h, int) and h == 0 and not uses:
                    pe.wait_ge(qk_lo, NC)
                    return
                _, kind, n, b, part = uses[-1] if uses else SHARED_USE[-1]
                n = h + n if uses else h - 1
                if kind == "qk":
                    pe.wait_ge(qk_lo, n * (2 * B) + 2 * b + part + 1)
                else:
                    pe.wait_ge(wo_scaled, n * (B * NC) + b * NC + part + 1)

            def scores(h, s):
                b, i = divmod(s, QB)
                if i == 0:
                    pe.wait_ge(k_copied[b], h * 16 + 16)
                if not (isinstance(h, int) and h == 0 and s < CH):
                    pe.wait_ge(probs_ready, h * S + s - i + scores_before(i))
                q = q_hl[b][:, i * P:(i + 1) * P]
                n = P * (i + 1 + (i % CH == 0))
                at = 0
                for end in [n] if n <= W else [W, n]:
                    for part in range(2):
                        last = pe.matmul(scores_of(i)[:, at:end], q, k_hl[b][:, part, at:end],
                                         start=part == 0, stop=part == 1)
                    at = end
                last.then_inc(scores_ready, 1)

            def transpose_probs(h, s, g):
                i = s % QB
                k = group_of(s, g)
                if g == 0:
                    pe.wait_ge(probs_ready, h * S + s + 1)
                if not (isinstance(h, int) and h == 0 and k < 2):
                    pe.wait_ge(pT_ready, h * G_HEAD + k - 1)
                for j in range(CH * g, min(CH * (g + 1), i + 1)):
                    o = (j - CH * g) * P
                    last = pe.transpose(trans_ps[k % 2][:, o:o + P], probs[s % 4][:, j * P:(j + 1) * P], ident[:])
                last.then_inc(pT_psum, 1)

            def values(h, b, c, j0, j1):
                u = h * (B * NC) + b * NC + c
                nk = CH * (c + 1)
                if j0 == 0:
                    pe.wait_ge(pT_ready, h * G_HEAD + group_of(QB * b + CH * c + CH - 1, c) + 1)
                    if c == 0:
                        pe.wait_ge(v_ready, h * B + b + 1)
                    if isinstance(u, int) and u == 0:
                        pe.wait_ge(zeros_ready, 2 * NC)
                    else:
                        pe.wait_ge(oT_ready, u)
                for j in range(j0, j1):
                    q0 = min(max(0, j - CH * c), CH - 2) * P
                    for part in (pT_hi, pT_lo):
                        last = pe.matmul(out_ps[:, q0:W], v_hl[b][:, j, :], part[c][:, j, q0:W],
                                         start=j == 0 and part is pT_hi, stop=j == nk - 1 and part is pT_lo)
                if j1 == nk:
                    last.then_inc(oT_psum, 1)

            def project_out(h, b, c, j0, j1):
                if j0 == 0:
                    pe.wait_ge(oT_ready, h * (B * NC) + b * NC + c + 1)
                for j in range(j0, j1):
                    last = pe.matmul(shared_ps[:, j * P:(j + 1) * P], oT[c][:, j * P:(j + 1) * P],
                                     wo[:, h, :], start=True, stop=True)
                if j1 == CH:
                    last.then_inc(wo_psum, 1)

            def fillers(h, s, last):
                first = isinstance(h, int) and h == 0
                pieces = []
                for n, at in ((h - 1, s + S), (h, s)):
                    if at >= S and first:
                        continue
                    if at in PV_SLOT:
                        b, c, j0, j1 = PV_SLOT[at]
                        pieces += [lambda n=n, b=b, c=c, j=j: values(n, b, c, j, j + 1) for j in range(j0, j1)]
                    if at in WO_SLOT:
                        b, c = WO_SLOT[at]
                        pieces.append(lambda n=n, b=b, c=c: (wait_shared(h, s, last), project_out(n, b, c, 0, 2)))
                        pieces.append(lambda n=n, b=b, c=c: project_out(n, b, c, 2, CH))
                if s in QK_SLOT:
                    nxt, b, half = QK_SLOT[s]
                    if not (nxt and last):
                        pieces.append(lambda: (wait_shared(h, s, last), project_qk(h + nxt, b, half)))
                return pieces

            def slot(h, s, carried, last):
                scores(h, s)
                pieces = fillers(h, s, last)
                n, t = (h, s - LAG_PE) if s >= LAG_PE else (h - 1, s - LAG_PE + S)
                if s >= LAG_PE or carried:
                    for g in range(GROUPS[t % QB]):
                        transpose_probs(n, t, g)
                        if pieces:
                            pieces.pop(0)()
                for piece in pieces:
                    piece()

            for r in range(2):
                pe.wait_ge((v_evac_act, v_evac_dve)[r], NB)
            pe.wait_ge(wo_loaded, 32)
            for s in range(S):
                slot(0, s, False, False)
            with pe.Fori(1, H - 1) as h:
                for s in range(S):
                    slot(h, s, True, False)
            for s in range(S):
                slot(H - 1, s, True, True)
            carried_uses = sorted(t for t in WO_SLOT if t >= S)
            for s in range(S, TAIL):
                if s - LAG_PE < S:
                    for g in range(GROUPS[(s - LAG_PE) % QB]):
                        transpose_probs(H - 1, s - LAG_PE, g)
                if s in PV_SLOT:
                    values(H - 1, *PV_SLOT[s])
                if s in WO_SLOT:
                    pe.wait_ge(wo_scaled, H * B * NC - len(carried_uses) + carried_uses.index(s))
                    project_out(H - 1, *WO_SLOT[s], 0, CH)

            def logits():
                pe.wait_ge(wr_ready, 1)
                pe.wait_ge(nT_ready, 2 * NCH)
                for t in range(NB):
                    rows = slice(t * P, (t + 1) * P)
                    last = three(out_ps[:, t * E:(t + 1) * E], nT_hi[:, rows], nT_lo[:, rows], wr_hi[:], wr_lo[:])
                last.then_inc(logit_psum, 1)

            def hidden_units(e, c, i):
                for k in range(HB):
                    if not (isinstance(e, int) and e == 0 and c == 0):
                        pe.wait_ge(hidden_ready, e * (NCH * HB) + (c - 1) * HB + k + 1)
                    ws, ts = slice(k * P, (k + 1) * P), slice(c * W, (c + 1) * W)
                    three(banks[k], wfc_hi[i][:, ws], wfc_lo[i][:, ws], nT_hi[:, ts], nT_lo[:, ts])\
                        .then_inc(fc_psum, 1)

            def second_layer(e, c, i):
                pe.wait_ge(hidden_ready, e * (NCH * HB) + c * HB + HB)
                if not (isinstance(e, int) and e == 0 and c < 2):
                    pe.wait_ge(moe_added, e * NCH + c - 1)
                for j in range(CH):
                    for k in range(HB):
                        o = (k % 2) * W + j * P
                        last = pe.matmul(trans_ps[c % 2][:, j * P:(j + 1) * P], hidden[c % 2][k // 2][:, o:o + P],
                                         wproj[i][:, k, :], start=k == 0, stop=k == HB - 1)
                last.then_inc(moe_psum, 1)

            def expert(e, i, before):
                pe.wait_ge(wfc_ready, e + 1)
                for c in range(NCH):
                    hidden_units(e, c, i)
                    if c:
                        second_layer(e, c - 1, i)
                    else:
                        second_layer(before, NCH - 1, 1 - i)

            def transpose_gates():
                pe.wait_ge(gate_ready, 1)
                for c in range(NCH):
                    last = pe.transpose(out_ps[0:CH * NE, c * P:(c + 1) * P],
                                        gate[:, CH * c:CH * (c + 1), :].rearrange("p j e -> p (j e)"), ident[:])
                last.then_inc(gate_T_psum, 1)

            def gated_biases(c):
                pe.wait_ge(gate_T_ready, 1)
                if c >= 2:
                    pe.wait_ge(bias_added, c - 1)
                pe.matmul((shared_ps, out_ps)[c % 2][:], gate_T[:, c, :], bproj_blocks[:],
                          start=True, stop=True).then_inc(bias_psum, 1)

            for c in range(NC):
                transposes(1, c)
            pe.wait_ge(wo_scaled, H * B * NC)
            pe.wait_ge(small_loaded, 16 * (3 + 2 * CH))
            pe.transpose(shared_ps[:, 0:NE * HB], bfc_rows[:], ident[0:NE * HB, 0:NE * HB]).then_inc(bfc_T_psum, 1)
            pe.wait_ge(wfc_ready, 1)
            for c in range(NC):
                pe.wait_ge(nT_ready, NCH + c + 1)
                hidden_units(0, c, 0)
            for c in range(NC, NCH):
                transposes(1, c)
            pe.wait_ge(nT_ready, 2 * NCH)
            second_layer(0, 0, 0)
            logits()
            hidden_units(0, 2, 0)
            second_layer(0, 1, 0)
            transpose_gates()
            hidden_units(0, 3, 0)
            gated_biases(0)
            gated_biases(1)
            second_layer(0, 2, 0)
            gated_biases(2)
            gated_biases(3)
            with pe.Fori(1, NE - 1, 2) as e:
                expert(e, 1, e - 1)
                expert(e + 1, 0, e)
            second_layer(NE - 1, NCH - 1, 0)


_INS = ["L0_attn_x", "L0_attn_Wq", "L0_attn_Wk", "L0_attn_Wv", "L0_attn_Wo", "L0_attn_bo",
        "L0_attn_rel_pos_bias", "L0_ffn_Wfc_s", "L0_ffn_bfc_s", "L0_ffn_Wproj_s", "L0_ffn_bproj_s",
        "L0_ffn_Wr", "L0_ffn_Wfc", "L0_ffn_bfc", "L0_ffn_Wproj", "L0_ffn_bproj"]


def kernel(**inputs):
    import numpy as _np
    import concourse.bacc as _bacc
    from concourse import mybir as _mybir
    from concourse.bass_utils import run_bass_kernel_spmd as _run

    nc = _bacc.Bacc("TRN2", target_bir_lowering=False, num_devices=1)
    arrays, args = {}, []
    for name in _INS:
        a = _np.ascontiguousarray(inputs[name])
        arrays[f"in_{name}"] = a
        args.append(nc.dram_tensor(f"in_{name}", a.shape, _mybir.dt.from_np(a.dtype), kind="ExternalInput").ap())
    shape = inputs["L0_attn_x"].shape
    args.append(nc.dram_tensor("out_0", shape, _mybir.dt.float32, kind="ExternalOutput").ap())
    transformer_block(nc, *args)
    r = _run(nc, [arrays], core_ids=[0])
    return r.results[0]["out_0"]
```

```python
from contextlib import ExitStack

import concourse.bass as bass
from concourse import mybir


def transformer_block(
    nc: bass.Bass,
    x: bass.AP,
    Wq: bass.AP,
    Wk: bass.AP,
    Wv: bass.AP,
    Wo: bass.AP,
    bo: bass.AP,
    rel_pos_bias: bass.AP,
    Wfc_s: bass.AP,
    bfc_s: bass.AP,
    Wproj_s: bass.AP,
    bproj_s: bass.AP,
    Wr: bass.AP,
    Wfc: bass.AP,
    bfc: bass.AP,
    Wproj: bass.AP,
    bproj: bass.AP,
    out: bass.AP,
):
    f32 = mybir.dt.float32
    f32r = mybir.dt.float32r
    ALU = mybir.AluOpType
    ACT = mybir.ActivationFunctionType
    AX = mybir.AxisListType.X

    P = 128
    B, T, D = x.shape
    H, R = rel_pos_bias.shape
    HD = Wq.shape[1]
    DH = HD // H
    NB = B * T // P
    QB = T // P
    HI_BY_ACT = 3
    S = B * QB
    CH = 4
    W = CH * P
    NC = QB // CH
    E = Wr.shape[1]
    NE = E + 1
    HID = Wfc_s.shape[1]
    HB = HID // P
    NCH = NB // CH
    EPS = 1e-5
    MASKED = 1e30
    SCALE = -1.0 / DH
    assert (P, D, R, DH, B, NC) == (128, 128, 128, 64, 2, 2)

    LAG_PE = 2
    LAG_ACT = 2
    LAG_DVE = 2
    GROUPS = [1 if i < CH else 2 for i in range(QB)]
    G_UNIT = sum(GROUPS)
    G_HEAD = B * G_UNIT

    def group_of(s, g):
        return (s // QB) * G_UNIT + sum(GROUPS[: s % QB]) + g

    PV_SLOT = {}
    WO_SLOT = {}
    PV0 = [7, 8, 9, 9]
    PV1 = [11, 11, 11, 12, 13, 13, 14, 14]
    WO = [11, 15]
    QK = [0, 1]
    for _b in range(B):
        for _c, _pv in enumerate((PV0, PV1)):
            for _s in sorted(set(_pv)):
                PV_SLOT[QB * _b + _s] = (_b, _c, _pv.index(_s), len(_pv) - _pv[::-1].index(_s))
            WO_SLOT[QB * _b + WO[_c]] = (_b, _c)
    QK_SLOT = {QK[0]: (0, 1, 0), QK[1]: (0, 1, 1), QB + QK[0]: (1, 0, 0), QB + QK[1]: (1, 0, 1)}
    TAIL = max(WO_SLOT) + 1
    NORMS = ([(0, CH * c) for c in range(NCH)] + [(n, QB * b) for b in range(B) for n in (1, 2)]
             + [(3, CH * c) for c in range(NCH)])
    norms_to = lambda n, lo: NORMS.index((n, lo)) + 1
    SHARED_USE = sorted([(s, "qk", n, b, half) for s, (n, b, half) in QK_SLOT.items()]
                        + [(s % S, "wo", -(s // S), b, c) for s, (b, c) in WO_SLOT.items()])

    assert len({u[0] for u in SHARED_USE}) == len(SHARED_USE)
    N_TURN = H * 2 * P // W

    v_dram = nc.dram_tensor("v_scratch", (B * T, HD), f32, kind="Internal").ap()
    gate_dram = nc.dram_tensor("gate_scratch", (E, B * T), f32, kind="Internal").ap()
    bias_dram = nc.dram_tensor("bias_scratch", (H, 3 * P), f32, kind="Internal").ap()

    ctx = ExitStack()
    with ctx:
        def sb(name, shape, dt=f32):
            return ctx.enter_context(nc.sbuf_tensor(name, shape, dt))

        def pb(name, shape):
            return ctx.enter_context(nc.psum_tensor(name, shape, f32))

        def sem(name):
            return ctx.enter_context(nc.semaphore(name))

        x_sb = sb("x_sb", [P, NB, D])
        normed = sb("normed", [P, NB, D])
        acc = sb("acc", [P, NB, D])
        nT_hi = sb("nT_hi", [P, B * T], f32r)
        nT_lo = sb("nT_lo", [P, B * T], f32r)
        wqk = sb("wqk", [P, H, 2 * DH])
        wqk_hl = sb("wqk_hl", [P, 4 * DH], f32r)
        wqk_hi, wqk_lo = wqk_hl[:, 0:2 * DH], wqk_hl[:, 2 * DH:4 * DH]
        wv = sb("wv", [P, HD])
        wo = sb("wo", [P, H, D])
        rel = sb("rel", [H, R])
        bias_line = sb("bias_line", [H, 3 * P])
        bias_all = sb("bias_all", [P, H, 2 * P])
        bias_b = [sb(f"bias_{b}", [P, T]) for b in range(B)]
        q_hl = [sb(f"q_hl{b}", [P, T], f32r) for b in range(B)]
        k_hl = [sb(f"k_hl{b}", [P, 2, T], f32r) for b in range(B)]
        v_raw = [sb(f"v_raw{b}", [P, QB, DH]) for b in range(B)]
        v_hl = [sb(f"v_hl{b}", [P, QB, 2 * DH], f32r) for b in range(B)]
        probs = [sb(f"probs{r}", [P, T]) for r in range(4)]
        pT_hi = [sb(f"pT_hi{c}", [P, CH * (c + 1), W], f32r) for c in range(NC)]
        pT_lo = [sb(f"pT_lo{c}", [P, CH * (c + 1), W], f32r) for c in range(NC)]
        oT = [sb(f"oT{c}", [P, W]) for c in range(NC)]
        head_out = [sb(f"head_out{c}", [P, W]) for c in range(NC)]
        row_min = sb("row_min", [P, S])
        row_sum = sb("row_sum", [P, S])
        row_inv = sb("row_inv", [P, S])
        ident = sb("ident", [P, P])
        exchange = sb("exchange", [P, P])
        stats = sb("stats", [P, NB, 6])
        mv = sb("mv", [P, NB, 2])
        var_eps = sb("var_eps", [P, NB])
        std = sb("std", [P, NB])
        newton = sb("newton", [P, NB])
        rstd = sb("rstd", [P, NB])
        wv_hi = pT_hi[1][:, 0:2, :].rearrange("p a b -> p (a b)")
        wv_lo = pT_lo[1][:, 0:2, :].rearrange("p a b -> p (a b)")
        wfc_raw = [v_raw[i][:].rearrange("p a b -> p (a b)") for i in range(2)]
        wfc_hi = [pT_hi[0][:, i, :] for i in range(2)]
        wfc_lo = [pT_lo[0][:, i, :] for i in range(2)]
        wproj_raw = [bias_b[i][:, 0:HB * D].rearrange("p (k d) -> p k d", d=D) for i in range(2)]
        wproj_hi = [pT_hi[0][:, 2 + i, :].rearrange("p (k d) -> p k d", d=D) for i in range(2)]
        wproj_lo = [pT_lo[0][:, 2 + i, :].rearrange("p (k d) -> p k d", d=D) for i in range(2)]
        layer_bias = sb("layer_bias", [NE * HB + NE, P])
        layer_bias_T = sb("layer_bias_T", [P, NE * HB + NE])
        hidden = [[probs[2 * i + k // 2][:, (k % 2) * W:(k % 2 + 1) * W] for k in range(HB)] for i in range(2)]
        hidden_hi = [[pT_hi[1][:, HB * i + k, :] for k in range(HB)] for i in range(2)]
        hidden_lo = [[pT_lo[1][:, HB * i + k, :] for k in range(HB)] for i in range(2)]
        wr = sb("wr", [P, E])
        wr_hi, wr_lo = wqk_hl[:, 0:E], wqk_hl[:, E:2 * E]
        logit = sb("logit", [P, NB, E])
        rank = sb("rank", [P, NB, E])
        pick = [sb(f"pick{i}", [P, NB, E]) for i in range(2)]
        order = sb("order", [P, E])
        top = [sb(f"top{i}", [P, NB]) for i in range(2)]
        first = sb("first", [P, NB])
        gate = sb("gate", [P, NB, E])
        gate_T = wqk[0:CH * E, 0:CH, :]
        gate_rows = [bias_all[:, i * (B * T // (2 * P)):(i + 1) * (B * T // (2 * P)), :].rearrange("p h c -> p (h c)")
                     for i in range(2)]
        gated = [head_out[c] for c in range(2)]
        acc_T = acc[:].rearrange("p t d -> p (t d)")
        offset = sb("offset", [P, NB])
        shift = sb("shift", [P, NB])

        score_ps = pb("score_ps", [P, 2 * T])
        trans_ps = [pb(f"trans_ps{r}", [P, W]) for r in range(2)]
        out_ps = pb("out_ps", [P, W])
        shared_ps = pb("shared_ps", [P, W])
        banks = [score_ps[:, r * W:(r + 1) * W] for r in range(4)]
        moe_out = [shared_ps[:], out_ps[:], banks[0], banks[1]]

        def scores_at(i):
            return P if i == CH else 0

        def scores_of(i):
            return score_ps[:, i * W:(i + 1) * W] if i < CH else score_ps[:, (i % 2) * T + scores_at(i):(i % 2 + 1) * T]

        def scores_before(i):
            banks_of = lambda j: {j} if j < CH else {2 * (j % 2), 2 * (j % 2) + 1}
            return max(j for j in range(i - QB, i) if banks_of(j % QB) & banks_of(i)) + 1

        act_passed = sem("act_passed")
        dve_passed = sem("dve_passed")
        pool_passed = sem("pool_passed")
        x_loaded = [sem(f"x_loaded{c}") for c in range(NCH)]
        wqk_loaded = sem("wqk_loaded")
        wv_loaded = sem("wv_loaded")
        wo_loaded = sem("wo_loaded")
        rel_loaded = sem("rel_loaded")
        small_loaded = sem("small_loaded")
        bias_line_stored = sem("bias_line_stored")
        bias_loaded = sem("bias_loaded")
        bias_turn_psum = sem("bias_turn_psum")
        bias_turned = sem("bias_turned")
        ident_ready = sem("ident_ready")
        pool_done = sem("pool_done")
        dve_done = sem("dve_done")
        wqk_scaled = sem("wqk_scaled")
        wv_hi_done = sem("wv_hi_done")
        wv_split = sem("wv_split")
        var_ready = sem("var_ready")
        std_ready = sem("std_ready")
        normed_ready = sem("normed_ready")
        moe_in_ready = sem("moe_in_ready")
        offset_ready = sem("offset_ready")
        out_normed = sem("out_normed")
        nT_psum = sem("nT_psum")
        nT_hi_ready = sem("nT_hi_ready")
        nT_ready = sem("nT_ready")
        v_psum = sem("v_psum")
        v_evac_act = sem("v_evac_act")
        v_evac_dve = sem("v_evac_dve")
        v_stored = [sem(f"v_stored{r}") for r in range(4)]
        zeros_ready = sem("zeros_ready")
        wqk_hi_done = sem("wqk_hi_done")
        wqk_ready = sem("wqk_ready")
        bias_ready = sem("bias_ready")
        v_loaded = [sem(f"v_loaded{b}") for b in range(B)]
        v_hi_done = sem("v_hi_done")
        v_ready = sem("v_ready")
        qk_psum = sem("qk_psum")
        qk_hi = sem("qk_hi")
        qk_lo = sem("qk_lo")
        q_copied = [sem(f"q_copied{b}") for b in range(B)]
        acc_started = sem("acc_started")
        acc_added = sem("acc_added")
        k_copied = [sem(f"k_copied{b}") for b in range(B)]
        scores_ready = sem("scores_ready")
        far_zeroed = sem("far_zeroed")
        min_ready = sem("min_ready")
        probs_ready = sem("probs_ready")
        pT_psum = sem("pT_psum")
        pT_hi_ready = sem("pT_hi_ready")
        pT_ready = sem("pT_ready")
        inv_ready = sem("inv_ready")
        oT_psum = sem("oT_psum")
        oT_ready = sem("oT_ready")
        wo_psum = sem("wo_psum")
        wo_scaled = sem("wo_scaled")
        moe_w_loaded = [sem(f"moe_w_loaded{i}") for i in range(2)]
        wfc_hi_done = sem("wfc_hi_done")
        wfc_ready = sem("wfc_ready")
        wr_ready = sem("wr_ready")
        logit_psum = sem("logit_psum")
        exp_ready = sem("exp_ready")
        logit_ready = sem("logit_ready")
        gate_ready = sem("gate_ready")
        gate_T_psum = sem("gate_T_psum")
        gate_T_ready = sem("gate_T_ready")
        layer_bias_psum = sem("layer_bias_psum")
        layer_bias_ready = sem("layer_bias_ready")
        fc_psum = sem("fc_psum")
        wproj_hi_done = sem("wproj_hi_done")
        wproj_ready = sem("wproj_ready")
        hidden_ready = sem("hidden_ready")
        hidden_hi_act = sem("hidden_hi_act")
        hidden_hi_dve = sem("hidden_hi_dve")
        hidden_lo_ready = sem("hidden_lo_ready")
        moe_psum = sem("moe_psum")
        gated_ready = sem("gated_ready")
        moe_added = sem("moe_added")
        gates_stored = sem("gates_stored")
        gates_loaded = [sem(f"gates_loaded{i}") for i in range(2)]
        moe_out_psum = sem("moe_out_psum")
        result_ready = sem("result_ready")
        result_stored = sem("result_stored")

        block = ctx.enter_context(nc.Block())
        x_blocks = x.rearrange("b (t p) d -> p (b t) d", p=P)
        out_blocks = out.rearrange("b (t p) d -> p (b t) d", p=P)

        @block.sync
        def _(sp):
            for c in range(NCH):
                sp.dma_start(x_sb[:, CH * c:CH * (c + 1), :],
                             x_blocks[:, CH * c:CH * (c + 1), :]).then_inc(x_loaded[c], 16)

            sp.wait_ge(dve_done, 2)
            sp.dma_start(bias_dram, bias_line[:]).then_inc(bias_line_stored, 16)
            sp.wait_ge(bias_line_stored, 16)
            sp.dma_start(bias_all[:], bass.AP(bias_dram.tensor, 0, [[1, P], [3 * P, H], [1, 2 * P]]))\
              .then_inc(bias_loaded, 16)

            def store_v(t):
                sp.wait_ge(v_evac_act, t + 1)
                sp.wait_ge(v_evac_dve, t + 1)
                sp.dma_start(v_dram[t * P:(t + 1) * P, :], probs[t % 4][:]).then_inc(v_stored[t % 4], 16)

            def load_v(h, b):
                src = bass.AP(v_dram.tensor, h * DH + b * T * HD, [[HD, P], [P * HD, QB], [1, DH]])
                sp.dma_start(v_raw[b][:], src).then_inc(v_loaded[b], 16)

            def place_q(h, b):
                sp.wait_ge(qk_lo, h * (2 * B) + 2 * b + 2)
                for part in range(2):
                    sp.dma_start(q_hl[b][part * DH:(part + 1) * DH, :].bitcast(f32),
                                 k_hl[b][0:DH, part, :].bitcast(f32)).then_inc(q_copied[b], 16)

            def place_k(h, b):
                sp.wait_ge(q_copied[b], h * 32 + 32)
                sp.dma_start(k_hl[b][0:DH, :, :].bitcast(f32), k_hl[b][DH:P, :, :].bitcast(f32))\
                  .then_inc(k_copied[b], 16)

            def head(h, last=False):
                if not (isinstance(h, int) and h == 0):
                    sp.wait_ge(v_ready, h * B)
                load_v(h, 1)
                place_q(h, 1)
                place_k(h, 1)
                if not last:
                    sp.wait_ge(v_ready, h * B + 1)
                    load_v(h + 1, 0)
                    place_q(h + 1, 0)
                    place_k(h + 1, 0)

            for t in range(NB):
                store_v(t)
                if t == 5:
                    place_q(0, 0)
                if t == 7:
                    place_k(0, 0)
            for r in range(4):
                sp.wait_ge(v_stored[r], 16 * (NB // 4))
            load_v(0, 0)
            head(0)
            with sp.Fori(1, H - 1) as h:
                head(h)
            head(H - 1, last=True)

            def load_expert(i, wf, wp):
                sp.dma_start(wfc_raw[i], wf).then_inc(moe_w_loaded[i], 16)
                sp.dma_start(wproj_raw[i], wp).then_inc(moe_w_loaded[i], 16)

            sp.wait_ge(v_ready, (H - 1) * B + 1)
            sp.wait_ge(min_ready, (H - 1) * S + QB)
            load_expert(0, Wfc_s, Wproj_s.rearrange("(k p) n -> p k n", p=P))
            sp.wait_ge(v_ready, H * B)
            sp.wait_ge(min_ready, H * S)
            load_expert(1, Wfc[0, :, :], Wproj[0, :, :].rearrange("(k p) n -> p k n", p=P))

            def expert_src(e):
                return (bass.AP(Wfc.tensor, (e - 1) * (D * HID), [[HID, P], [1, HID]]),
                        bass.AP(Wproj.tensor, (e - 1) * (D * HID), [[D, P], [P * D, HB], [1, D]]))

            def reload(e, i):
                sp.wait_ge(wproj_ready, e - 1)
                load_expert(i, *expert_src(e))

            def load_gates(e, i):
                if not (isinstance(e, int) and e <= 2):
                    sp.wait_ge(gated_ready, (e - 1) * NCH)
                sp.dma_start(gate_rows[i], bass.AP(gate_dram.tensor, (e - 1) * (B * T), [[0, P], [1, B * T]]))\
                  .then_inc(gates_loaded[i], 16)

            reload(2, 0)
            sp.wait_ge(gate_T_ready, 1)
            for j in range(CH):
                sp.dma_start(bass.AP(gate_dram.tensor, j * P, [[B * T, E], [W, NCH], [1, P]]),
                             gate_T[j * E:(j + 1) * E, :, :]).then_inc(gates_stored, 16)
            sp.wait_ge(gates_stored, 16 * CH)
            load_gates(1, 1)
            load_gates(2, 0)
            with sp.Fori(3, NE - 1, 2) as e:
                for i in range(2):
                    reload(e + i, 1 - i)
                    load_gates(e + i, 1 - i)

            for c in range(NCH):
                sp.wait_ge(result_ready, c + 1)
                sp.dma_start(out_blocks[:, CH * c:CH * (c + 1), :],
                             normed[:, CH * c:CH * (c + 1), :]).then_inc(result_stored, 16)
            sp.wait_ge(result_stored, 16 * NCH)

        @block.gpsimd
        def _(pool):
            own = [0]

            def then_wait(ins):
                own[0] += 1
                ins.then_inc(pool_done, 1)
                pool.wait_ge(pool_done, own[0])

            then_wait(pool.memset(ident[:], 0.0))
            pool.affine_select(out=ident[:], in_=ident[:], compare_op=ALU.not_equal, fill=1.0, base=0,
                               pattern=[[-1, P]], channel_multiplier=1).then_inc(ident_ready, 1)
            then_wait(pool.memset(exchange[:], 0.0))
            pool.affine_select(out=exchange[:], in_=exchange[:], compare_op=ALU.not_equal, fill=1.0,
                               base=1 - P, pattern=[[1, P]], channel_multiplier=1).then_inc(ident_ready, 1)

            def split_wqk(h):
                pool.sem_inc(pool_passed, 1)
                pool.tensor_copy(wqk_hi, wqk[:, h, :]).then_inc(wqk_hi_done, 1)
                pool.wait_ge(wqk_hi_done, h + 1)
                pool.sem_inc(pool_passed, 1)
                pool.tensor_tensor(wqk_lo, wqk[:, h, :], wqk_hi, ALU.subtract).then_inc(wqk_ready, 1)

            def take_bias(h, b):
                pool.sem_inc(pool_passed, 1)
                pool.tensor_copy(bias_b[b][:, T - 2 * P:T], bias_all[:, h, :]).then_inc(bias_ready, 1)

            def zero_pads():
                for c in range(NC):
                    for part in (pT_hi, pT_lo):
                        zero = part[c][:, CH * c + CH - 1, (CH - 2) * P:(CH - 1) * P]
                        pool.tensor_scalar(zero, ident[:], 0.0, None, ALU.mult).then_inc(zeros_ready, 1)

            def split_v(h, b):
                n = h * B + b
                pool.wait_ge(v_loaded[b], h * 16 + 16)
                pool.sem_inc(pool_passed, 1)
                pool.tensor_copy(v_hl[b][:, :, 0:DH], v_raw[b][:]).then_inc(v_hi_done, 1)
                pool.wait_ge(v_hi_done, n + 1)
                pool.tensor_tensor(v_hl[b][:, :, DH:2 * DH], v_raw[b][:], v_hl[b][:, :, 0:DH],
                                   ALU.subtract).then_inc(v_ready, 1)

            def add_head(h, b, c):
                n = h * (B * NC) + b * NC + c
                pool.wait_ge(wo_scaled, n + 1)
                if isinstance(n, int) and n == 0:
                    pool.wait_ge(acc_started, 16)
                else:
                    pool.wait_ge(acc_added, n)
                blocks = slice(QB * b + CH * c, QB * b + CH * (c + 1))
                pool.tensor_tensor(acc[:, blocks, :], acc[:, blocks, :],
                                   head_out[c][:].rearrange("p (t d) -> p t d", d=D), ALU.add)\
                    .then_inc(acc_added, 1)

            def slot(h, s, carried, last):
                if carried and s + S in WO_SLOT:
                    add_head(h - 1, *WO_SLOT[s + S])
                if s in WO_SLOT:
                    add_head(h, *WO_SLOT[s])
                if s == 1:
                    if carried:
                        pool.wait_ge(min_ready, h * S)
                    take_bias(h, 1)
                if s == 5:
                    pool.wait_ge(qk_psum, h * (2 * B) + 2 * B)
                    if not last:
                        split_wqk(h + 1)
                    if carried:
                        pool.wait_ge(oT_psum, h * (B * NC))
                    split_v(h, 1)
                if s == QB - 2 and not carried:
                    for r in range(2):
                        pool.dma_start(wo[r * DH:(r + 1) * DH, :, :],
                                       Wo.rearrange("(h d) n -> d h n", h=H)).then_inc(wo_loaded, 16)
                    pool.dma_start(acc[:], bass.AP(bo.tensor, 0, [[0, P], [0, NB], [1, D]])).then_inc(acc_started, 16)
                if s == QB and not last:
                    pool.wait_ge(min_ready, h * S + QB)
                    take_bias(h + 1, 0)
                if s == QB + 5 and not last:
                    pool.wait_ge(oT_psum, h * (B * NC) + NC)
                    split_v(h + 1, 0)

            pool.wait_ge(wv_hi_done, 1)
            pool.tensor_tensor(wv_lo, wv[:], wv_hi, ALU.subtract).then_inc(wv_split, 1)
            for b in range(B):
                pool.memset(bias_b[b][:, 0:T - 2 * P], 0.0).then_inc(far_zeroed, 1)
            pool.wait_ge(wqk_loaded, 32)
            pool.wait_ge(wqk_scaled, 1)
            split_wqk(0)
            zero_pads()

            pool.dma_start(wr[:], Wr).then_inc(small_loaded, 16)
            for first_row, biases in ((0, bfc_s.rearrange("(k p) -> k p", p=P)),
                                      (HB, bfc.rearrange("e (k p) -> (e k) p", p=P)),
                                      (NE * HB, bproj_s.rearrange("(a n) -> a n", a=1)),
                                      (NE * HB + 1, bproj)):
                pool.dma_start(layer_bias[first_row:first_row + biases.shape[0], :], biases)\
                    .then_inc(small_loaded, 16)

            pool.wait_ge(bias_turned, N_TURN)
            take_bias(0, 0)
            split_v(0, 0)
            for s in range(S):
                slot(0, s, False, False)
            with pool.Fori(1, H - 1) as h:
                for s in range(S):
                    slot(h, s, True, False)
            for s in range(S):
                slot(H - 1, s, True, True)
            def split_wfc(e, i):
                pool.wait_ge(moe_w_loaded[i], (e - i) * 16 + 32)
                if not (isinstance(e, int) and e < 2):
                    pool.wait_ge(fc_psum, (e - 1) * (NCH * HB))
                pool.sem_inc(pool_passed, 1)
                pool.tensor_copy(wfc_hi[i], wfc_raw[i]).then_inc(wfc_hi_done, 1)
                pool.wait_ge(wfc_hi_done, e + 1)
                pool.tensor_tensor(wfc_lo[i], wfc_raw[i], wfc_hi[i], ALU.subtract).then_inc(wfc_ready, 1)

            def split_wproj(e, i):
                if not (isinstance(e, int) and e < 2):
                    pool.wait_ge(moe_psum, (e - 1) * NCH)
                pool.sem_inc(pool_passed, 1)
                pool.tensor_copy(wproj_hi[i], wproj_raw[i]).then_inc(wproj_hi_done, 1)
                pool.wait_ge(wproj_hi_done, e + 1)
                pool.tensor_tensor(wproj_lo[i], wproj_raw[i], wproj_hi[i], ALU.subtract).then_inc(wproj_ready, 1)

            def add_expert(e, c):
                pool.wait_ge(gated_ready, e * NCH + c + 1)
                if not (isinstance(e, int) and e == 1):
                    pool.wait_ge(moe_added, (e - 2) * NCH + c + 1)
                cols = slice(c * W, (c + 1) * W)
                pool.sem_inc(pool_passed, 1)
                pool.tensor_tensor(acc_T[:, cols], acc_T[:, cols], gated[c % 2][:], ALU.add).then_inc(moe_added, 1)

            def expert(e, i):
                split_wfc(e + 1, i)
                add_expert(e, 0)
                split_wproj(e + 1, i)
                for c in range(1, NCH):
                    add_expert(e, c)

            pool.wait_ge(small_loaded, 16 * 5)
            then_wait(pool.tensor_copy(wr_hi, wr[:]))
            pool.tensor_tensor(wr_lo, wr[:], wr_hi, ALU.subtract).then_inc(wr_ready, 1)
            for s in range(S, TAIL):
                if s in WO_SLOT:
                    if WO_SLOT[s] == (B - 1, NC - 1):
                        pool.wait_ge(oT_psum, H * B * NC - 1)
                        split_wfc(0, 0)
                    add_head(H - 1, *WO_SLOT[s])
            split_wproj(0, 0)
            split_wfc(1, 1)
            split_wproj(1, 1)
            expert(1, 0)
            with pool.Fori(2, NE - 2, 2) as e:
                expert(e, 1)
                expert(e + 1, 0)
            for c in range(NCH):
                add_expert(NE - 1, c)

        @block.scalar
        def _(act):
            act.dma_start(rel[:], rel_pos_bias).then_inc(rel_loaded, 16)
            act.dma_start(wv[:], Wv).then_inc(wv_loaded, 16)
            act.dma_start(wqk[:, :, 0:DH], Wq.rearrange("p (h d) -> p h d", h=H)).then_inc(wqk_loaded, 16)
            act.dma_start(wqk[:, :, DH:2 * DH], Wk.rearrange("p (h d) -> p h d", h=H)).then_inc(wqk_loaded, 16)

            def root(n, lo, hi):
                act.wait_ge(var_ready, norms_to(n, lo))
                act.activation(std[:, lo:hi], var_eps[:, lo:hi], ACT.Sqrt).then_inc(std_ready, 1)

            def nT_evac(n, c):
                act.wait_ge(nT_psum, n * NCH + c + 1)
                act.activation(nT_hi[:, c * W:(c + 1) * W], trans_ps[c % 2][:], ACT.Copy)\
                   .then_inc(nT_hi_ready, 1)

            def split_qk_hi(h, b, half):
                act.wait_ge(qk_psum, h * (2 * B) + 2 * b + half + 1)
                if not (isinstance(h, int) and h == 0):
                    act.wait_ge(scores_ready, h * S + QB * b + QB - S)
                act.activation(k_hl[b][:, 0, half * W:(half + 1) * W], shared_ps[:], ACT.Copy).then_inc(qk_hi, 1)

            def copy_v(t):
                act.wait_ge(v_psum, 2 * t + 1)
                if t >= 4:
                    act.wait_ge(v_stored[t % 4], 16 * (t // 4))
                act.activation(probs[t % 4][:, 0:W], banks[(2 * t) % 4], ACT.Copy).then_inc(v_evac_act, 1)

            root(0, 0, CH)
            act.wait_ge(wv_loaded, 16)
            act.activation(wv_hi, wv[:], ACT.Copy).then_inc(wv_hi_done, 1)
            root(0, CH, 2 * CH)
            nT_evac(0, 0)
            root(0, 2 * CH, 3 * CH)
            nT_evac(0, 1)
            act.wait_ge(wqk_loaded, 32)
            act.activation(wqk[:, :, 0:DH], wqk[:, :, 0:DH], ACT.Copy, scale=SCALE).then_inc(wqk_scaled, 1)
            copy_v(0)
            copy_v(1)
            root(0, 3 * CH, 4 * CH)
            nT_evac(0, 2)
            copy_v(2)
            copy_v(3)
            nT_evac(0, 3)
            split_qk_hi(0, 0, 0)
            copy_v(4)
            copy_v(5)
            split_qk_hi(0, 0, 1)
            act.activation(std[:], rstd[:], ACT.Exp)

            bias_flat = bias_all[:].rearrange("p h c -> p (h c)")
            for t in range(6, NB):
                copy_v(t)
                n = t - (NB - N_TURN)
                if n >= 0:
                    act.wait_ge(bias_turn_psum, n + 1)
                    act.activation(bias_flat[:, n * W:(n + 1) * W], trans_ps[n % 2][:], ACT.Copy)\
                       .then_inc(bias_turned, 1)

            def exp(h, s):
                n = P * (s % QB + 1)
                if isinstance(h, int) and h == 0 and s < 4:
                    act.wait_ge(v_stored[s], 16 * (NB // 4))
                act.wait_ge(min_ready, h * S + s + 1)
                act.activation(probs[s % 4][:, 0:n], scores_of(s % QB)[:, 0:n], ACT.Exp,
                               bias=row_min[:, s:s + 1], scale=-1.0,
                               accum_out=row_sum[:, s:s + 1]).then_inc(probs_ready, 1)

            def split_hi(h, s):
                b, i = divmod(s, QB)
                c, q = divmod(i, CH)
                u = h * (B * NC) + b * NC + c
                if q == 0 and not (isinstance(u, int) and u < NC):
                    act.wait_ge(oT_psum, u - (NC - 1))
                for g in range(GROUPS[i]):
                    k = group_of(s, g)
                    m = min(CH, i + 1 - CH * g)
                    act.wait_ge(pT_psum, h * G_HEAD + k + 1)
                    act.activation(pT_hi[c][:, CH * g:CH * g + m, q * P:(q + 1) * P],
                                   trans_ps[k % 2][:, 0:m * P].rearrange("p (m q) -> p m q", q=P),
                                   ACT.Copy).then_inc(pT_hi_ready, 1)

            def copy_oT(h, b, c, j0, j1):
                if j1 < CH * (c + 1):
                    return
                act.wait_ge(oT_psum, h * (B * NC) + b * NC + c + 1)
                act.activation(oT[c][:], out_ps[:], ACT.Copy).then_inc(oT_ready, 1)

            def slot(h, s, carried, last):
                if s >= LAG_ACT:
                    split_hi(h, s - LAG_ACT)
                elif carried:
                    split_hi(h - 1, s - LAG_ACT + S)
                if s in PV_SLOT:
                    copy_oT(h, *PV_SLOT[s])
                if carried and s + S in PV_SLOT:
                    copy_oT(h - 1, *PV_SLOT[s + S])
                exp(h, s)
                if s in QK_SLOT:
                    nxt, b, half = QK_SLOT[s]
                    if not (nxt and last):
                        split_qk_hi(h + nxt, b, half)

            for s in range(S):
                slot(0, s, False, False)
            with act.Fori(1, H - 1) as h:
                for s in range(S):
                    slot(h, s, True, False)
            for s in range(S):
                slot(H - 1, s, True, True)
            def normalise_moe_in(b):
                act.wait_ge(offset_ready, b + 1)
                for t in range(QB * b, QB * (b + 1)):
                    act.activation(normed[:, t, :], x_sb[:, t, :], ACT.Identity, bias=offset[:, t:t + 1],
                                   scale=rstd[:, t:t + 1]).then_inc(moe_in_ready, 1)

            for s in range(S, TAIL):
                if s - LAG_ACT < S:
                    split_hi(H - 1, s - LAG_ACT)
                if s in PV_SLOT:
                    if s == max(PV_SLOT):
                        root(1, 0, QB)
                    copy_oT(H - 1, *PV_SLOT[s])
            root(2, 0, QB)
            normalise_moe_in(0)
            for c in range(NC):
                nT_evac(1, c)
            root(1, QB, NB)

            def hidden_units(e, c):
                def high(k):
                    act.wait_ge(hidden_ready, e * (NCH * HB) + c * HB + k + 1)
                    if k == 0 and not (isinstance(e, int) and e == 0 and c < 2):
                        act.wait_ge(moe_psum, e * NCH + c - 1)
                    act.sem_inc(act_passed, 1)
                    act.activation(hidden_hi[c % 2][k], hidden[c % 2][k], ACT.Copy).then_inc(hidden_hi_act, 1)

                for k in range(HB):
                    act.wait_ge(fc_psum, e * (NCH * HB) + c * HB + k + 1)
                    if not (isinstance(e, int) and e == 0 and c < 2):
                        act.wait_ge(hidden_lo_ready, e * (NCH * HB) + (c - 2) * HB + k + 1)
                    act.sem_inc(act_passed, 1)
                    act.activation(hidden[c % 2][k], banks[k], ACT.Gelu_apprx_tanh,
                                   bias=layer_bias_T[:, bass.ds(e * HB + k, 1)]).then_inc(hidden_ready, 1)
                    if 0 < k <= HI_BY_ACT:
                        high(k - 1)

            act.wait_ge(layer_bias_psum, 1)
            act.activation(layer_bias_T[:], shared_ps[:, 0:NE * HB + NE], ACT.Copy).then_inc(layer_bias_ready, 1)
            act.wait_ge(layer_bias_ready, 1)
            hidden_units(0, 0)
            root(2, QB, NB)
            normalise_moe_in(1)
            for c in range(NC, NCH):
                nT_evac(1, c)
            hidden_units(0, 1)
            act.wait_ge(logit_ready, 1)
            act.activation(rank[:], logit[:], ACT.Exp).then_inc(exp_ready, 1)
            hidden_units(0, 2)
            hidden_units(0, 3)
            with act.Fori(1, NE) as e:
                for c in range(NCH):
                    hidden_units(e, c)

            for c in range(NCH):
                root(3, CH * c, CH * (c + 1))
                act.wait_ge(offset_ready, B + c + 1)
                for j in range(CH):
                    t = CH * c + j
                    last = act.activation(normed[:, t, :], moe_out[c][:, j * P:(j + 1) * P], ACT.Identity,
                                          bias=offset[:, t:t + 1], scale=rstd[:, t:t + 1])
                last.then_inc(out_normed, 1)

        @block.vector
        def _(dve):
            own = [0]

            def then_wait(ins):
                own[0] += 1
                ins.then_inc(dve_done, 1)
                dve.wait_ge(dve_done, own[0])

            dve.memset(bias_line[:, 0:P], 0.0)
            then_wait(dve.memset(bias_line[:, 2 * P:3 * P], MASKED))
            dve.wait_ge(rel_loaded, 16)
            then_wait(dve.tensor_scalar(bias_line[:, P:2 * P], rel[:], rel[:, 0:1], SCALE,
                                        ALU.subtract, ALU.mult))

            def moments(src, lo, hi, first=0):
                for t in range(lo, hi):
                    last = dve.bn_stats(stats[:, t, :], src[:, t - first, :])
                then_wait(last)
                for t in range(lo, hi):
                    last = dve.bn_aggr(mv[:, t, :], stats[:, t, :])
                then_wait(last)
                dve.tensor_scalar(var_eps[:, lo:hi], mv[:, lo:hi, 1], EPS, None, ALU.add).then_inc(var_ready, 1)

            def inverse_std(n, lo, hi):
                r, v, t = rstd[:, lo:hi], var_eps[:, lo:hi], newton[:, lo:hi]
                dve.wait_ge(std_ready, norms_to(n, lo))
                then_wait(dve.reciprocal(r, std[:, lo:hi]))
                then_wait(dve.tensor_tensor(t, r, r, ALU.mult))
                then_wait(dve.scalar_tensor_tensor(out=t, in0=t, scalar=-0.5, in1=v, op0=ALU.mult, op1=ALU.mult))
                then_wait(dve.scalar_tensor_tensor(out=r, in0=t, scalar=1.5, in1=r, op0=ALU.add, op1=ALU.mult))

            def normalise(dst, src, lo, hi):
                for t in range(lo, hi):
                    last = dve.tensor_scalar(dst[:, t, :], src[:, t, :], mv[:, t, 0:1], rstd[:, t:t + 1],
                                             ALU.subtract, ALU.mult)
                return last

            def nT_evac(n, c):
                dve.wait_ge(nT_hi_ready, n * NCH + c + 1)
                dve.tensor_tensor(nT_lo[:, c * W:(c + 1) * W], trans_ps[c % 2][:],
                                  nT_hi[:, c * W:(c + 1) * W], ALU.subtract).then_inc(nT_ready, 1)

            def split_qk_lo(h, b, half):
                cols = slice(half * W, (half + 1) * W)
                dve.wait_ge(qk_hi, h * (2 * B) + 2 * b + half + 1)
                dve.tensor_tensor(k_hl[b][:, 1, cols], shared_ps[:], k_hl[b][:, 0, cols],
                                  ALU.subtract).then_inc(qk_lo, 1)

            def copy_v(t):
                dve.wait_ge(v_psum, 2 * t + 2)
                if t >= 4:
                    dve.wait_ge(v_stored[t % 4], 16 * (t // 4))
                dve.tensor_copy(probs[t % 4][:, W:2 * W], banks[(2 * t + 1) % 4]).then_inc(v_evac_dve, 1)

            for c in range(NCH):
                dve.wait_ge(x_loaded[c], 16)
                moments(x_sb, CH * c, CH * (c + 1))
                inverse_std(0, CH * c, CH * (c + 1))
                normalise(normed, x_sb, CH * c, CH * (c + 1)).then_inc(normed_ready, 1)
                if c:
                    nT_evac(0, c - 1)
                if c >= 2:
                    copy_v(2 * c - 4)
                    copy_v(2 * c - 3)
            nT_evac(0, NCH - 1)
            split_qk_lo(0, 0, 0)
            copy_v(4)
            copy_v(5)
            split_qk_lo(0, 0, 1)
            for t in range(6, NB):
                copy_v(t)

            def row_minimum(h, s):
                b, i = divmod(s, QB)
                n = P * (i + 1)
                ps = scores_of(i)[:, 0:n]
                dve.wait_ge(scores_ready, h * S + s + 1)
                if i == 0:
                    dve.wait_ge(bias_ready, h * B + b + 1)
                    if isinstance(h, int) and h == 0:
                        dve.wait_ge(far_zeroed, B)
                dve.sem_inc(dve_passed, 1)
                dve.tensor_tensor_reduce(out=ps, in0=ps, in1=bias_b[b][:, T - n:T], scale=1.0, scalar=3e38,
                                         op0=ALU.add, op1=ALU.min,
                                         accum_out=row_min[:, s:s + 1]).then_inc(min_ready, 1)

            def split_lo(h, s):
                b, i = divmod(s, QB)
                c, q = divmod(i, CH)
                for g in range(GROUPS[i]):
                    k = group_of(s, g)
                    m = min(CH, i + 1 - CH * g)
                    dst = (slice(None), slice(CH * g, CH * g + m), slice(q * P, (q + 1) * P))
                    dve.wait_ge(pT_hi_ready, h * G_HEAD + k + 1)
                    dve.tensor_tensor(pT_lo[c][dst], trans_ps[k % 2][:, 0:m * P].rearrange("p (m q) -> p m q", q=P),
                                      pT_hi[c][dst], ALU.subtract).then_inc(pT_ready, 1)

            def invert_sums(h, b, c, j0, j1):
                if j0 > 0:
                    return
                s = QB * b + CH * c
                dve.wait_ge(probs_ready, h * S + s + CH)
                dve.reciprocal(row_inv[:, s:s + CH], row_sum[:, s:s + CH]).then_inc(inv_ready, 1)

            def scale_head(h, b, c):
                n = h * (B * NC) + b * NC + c
                dve.wait_ge(wo_psum, n + 1)
                dve.wait_ge(inv_ready, n + 1)
                if not (isinstance(n, int) and n < NC):
                    dve.wait_ge(acc_added, n - (NC - 1))
                blocks = slice(QB * b + CH * c, QB * b + CH * (c + 1))
                dve.tensor_tensor(head_out[c][:].rearrange("p (t d) -> p t d", d=D),
                                  shared_ps[:].rearrange("p (t d) -> p t d", d=D),
                                  row_inv[:, blocks].unsqueeze(2).broadcast_to([P, CH, D]),
                                  ALU.mult).then_inc(wo_scaled, 1)

            def slot(h, s, carried, last):
                row_minimum(h, s)
                if s >= LAG_DVE:
                    split_lo(h, s - LAG_DVE)
                elif carried:
                    split_lo(h - 1, s - LAG_DVE + S)
                for slots, do in ((PV_SLOT, invert_sums), (WO_SLOT, scale_head)):
                    if s in slots:
                        do(h, *slots[s])
                    if carried and s + S in slots:
                        do(h - 1, *slots[s + S])
                if s in QK_SLOT:
                    nxt, b, half = QK_SLOT[s]
                    if not (nxt and last):
                        split_qk_lo(h + nxt, b, half)

            for s in range(S):
                slot(0, s, False, False)
            with dve.Fori(1, H - 1) as h:
                for s in range(S):
                    slot(h, s, True, False)
            for s in range(S):
                slot(H - 1, s, True, True)
            def add_normed(b):
                lo, hi = QB * b, QB * (b + 1)
                inverse_std(1, lo, hi)
                dve.tensor_tensor(shift[:, lo:hi], mv[:, lo:hi, 0], rstd[:, lo:hi], ALU.mult)
                for t in range(lo, hi):
                    last = dve.scalar_tensor_tensor(out=x_sb[:, t, :], in0=acc[:, t, :],
                                                    scalar=rstd[:, t:t + 1], in1=x_sb[:, t, :],
                                                    op0=ALU.mult, op1=ALU.add)
                then_wait(last)
                moments(x_sb, lo, hi)

            def scale_and_offset(n, lo, hi):
                inverse_std(n, lo, hi)
                dve.scalar_tensor_tensor(out=offset[:, lo:hi], in0=mv[:, lo:hi, 0], scalar=-1.0,
                                         in1=rstd[:, lo:hi], op0=ALU.mult, op1=ALU.mult).then_inc(offset_ready, 1)

            for s in range(S, TAIL):
                if s - LAG_DVE < S:
                    split_lo(H - 1, s - LAG_DVE)
                if s in PV_SLOT:
                    invert_sums(H - 1, *PV_SLOT[s])
                if s == S + LAG_DVE - 1:
                    dve.wait_ge(acc_added, (H - 1) * B * NC + NC)
                    moments(acc, 0, QB)
                if s in WO_SLOT:
                    if s == max(WO_SLOT):
                        add_normed(0)
                    scale_head(H - 1, *WO_SLOT[s])
            scale_and_offset(2, 0, QB)
            dve.wait_ge(acc_added, H * B * NC)
            moments(acc, QB, NB)
            for c in range(NC):
                nT_evac(1, c)
            add_normed(1)
            scale_and_offset(2, QB, NB)

            def split_hidden(e, c):
                for k in range(HB):
                    raw, hi, lo = (a[c % 2][k] for a in (hidden, hidden_hi, hidden_lo))
                    if k == 0 and not (isinstance(e, int) and e == 0 and c < 2):
                        dve.wait_ge(moe_psum, e * NCH + c - 1)
                    if k < HI_BY_ACT:
                        dve.wait_ge(hidden_hi_act, (e * NCH + c) * HI_BY_ACT + k + 1)
                    else:
                        dve.wait_ge(hidden_ready, e * (NCH * HB) + c * HB + k + 1)
                        dve.sem_inc(dve_passed, 1)
                        dve.tensor_copy(hi, raw).then_inc(hidden_hi_dve, 1)
                        dve.wait_ge(hidden_hi_dve, (e * NCH + c) * (HB - HI_BY_ACT) + k - HI_BY_ACT + 1)
                    dve.sem_inc(dve_passed, 1)
                    dve.tensor_tensor(lo, raw, hi, ALU.subtract).then_inc(hidden_lo_ready, 1)

            def gate_expert(e, c, i):
                cols = slice(c * W, (c + 1) * W)
                bias = layer_bias_T[:, bass.ds(NE * HB + e, 1)]
                dve.wait_ge(moe_psum, e * NCH + c + 1)
                if isinstance(e, int) and e == 0:
                    dve.tensor_scalar(acc_T[:, cols], trans_ps[c % 2][:], bias, None, ALU.add)\
                       .then_inc(gated_ready, 1)
                    return
                if c == 0:
                    dve.wait_ge(gates_loaded[i], (e + i) * 8)
                if not (isinstance(e, int) and e == 1 and c < 2):
                    dve.wait_ge(moe_added, (e - 1) * NCH + c - 1)
                dve.sem_inc(dve_passed, 1)
                dve.scalar_tensor_tensor(out=gated[c % 2][:], in0=trans_ps[c % 2][:], scalar=bias,
                                         in1=gate_rows[i][:, cols], op0=ALU.add, op1=ALU.mult)\
                   .then_inc(gated_ready, 1)

            dve.wait_ge(layer_bias_ready, 1)
            split_hidden(0, 0)
            for c in range(NC, NCH):
                nT_evac(1, c)
            split_hidden(0, 1)

            for k in range(E):
                last = dve.memset(order[:, k:k + 1], float(E - k))
            then_wait(last)
            dve.wait_ge(logit_psum, 1)
            parts = out_ps[:, 0:2 * NB * E].rearrange("p (t h e) -> p t h e", h=2, e=E)
            each = lambda a: a.unsqueeze(2).broadcast_to([P, NB, E])
            then_wait(dve.tensor_copy(logit[:], parts[:, :, 1, :]))
            then_wait(dve.tensor_tensor(logit[:], parts[:, :, 0, :], logit[:], ALU.add))
            then_wait(dve.tensor_reduce(top[0][:], logit[:], AX, ALU.max))
            dve.tensor_tensor(logit[:], logit[:], each(top[0][:]), ALU.subtract).then_inc(logit_ready, 1)
            dve.wait_ge(exp_ready, 1)
            prefer = order[:].unsqueeze(1).broadcast_to([P, NB, E])
            for i in range(2):
                then_wait(dve.tensor_reduce(top[i][:], rank[:], AX, ALU.max))
                then_wait(dve.tensor_tensor(pick[i][:], rank[:], each(top[i][:]), ALU.is_equal))
                then_wait(dve.tensor_tensor(pick[i][:], pick[i][:], prefer, ALU.mult))
                then_wait(dve.tensor_reduce(first[:], pick[i][:], AX, ALU.max))
                then_wait(dve.tensor_tensor(pick[i][:], pick[i][:], each(first[:]), ALU.is_equal))
                if i == 0:
                    then_wait(dve.scalar_tensor_tensor(
                        out=rank[:].rearrange("p t e -> p (t e)"), in0=pick[0][:].rearrange("p t e -> p (t e)"),
                        scalar=-2.0, in1=rank[:].rearrange("p t e -> p (t e)"), op0=ALU.mult, op1=ALU.add))
            then_wait(dve.tensor_tensor(first[:], top[0][:], top[1][:], ALU.add))
            then_wait(dve.reciprocal(first[:], first[:]))
            for i in range(2):
                then_wait(dve.tensor_tensor(top[i][:], top[i][:], first[:], ALU.mult))
                then_wait(dve.tensor_tensor(pick[i][:], pick[i][:], each(top[i][:]), ALU.mult))
            dve.tensor_tensor(gate[:], pick[0][:], pick[1][:], ALU.add).then_inc(gate_ready, 1)

            gate_expert(0, 0, 0)
            split_hidden(0, 2)
            gate_expert(0, 1, 0)
            dve.wait_ge(gate_T_psum, 1)
            dve.tensor_copy(gate_T, out_ps[0:CH * E, :].rearrange("p (c q) -> p c q", q=P))\
               .then_inc(gate_T_ready, 1)
            split_hidden(0, 3)
            gate_expert(0, 2, 0)
            for t in range(NB):
                dve.tensor_scalar(x_sb[:, t, :], x_sb[:, t, :], shift[:, t:t + 1], None, ALU.subtract)

            def expert(e, i, before):
                for c in range(NCH):
                    split_hidden(e, c)
                    if c:
                        gate_expert(e, c - 1, i)
                    else:
                        gate_expert(before, NCH - 1, 1 - i)

            expert(1, 1, 0)
            with dve.Fori(2, NE - 2, 2) as e:
                expert(e, 0, e - 1)
                expert(e + 1, 1, e)

            def out_moments(c):
                dve.wait_ge(moe_out_psum, c + 1)
                moments(moe_out[c].rearrange("p (t d) -> p t d", d=D), CH * c, CH * (c + 1), CH * c)

            def add_x(c):
                lo, hi = CH * c, CH * (c + 1)
                dve.wait_ge(out_normed, c + 1)
                dve.tensor_tensor(normed[:, lo:hi, :], normed[:, lo:hi, :], x_sb[:, lo:hi, :], ALU.add)\
                   .then_inc(result_ready, 1)

            for c in range(NCH):
                split_hidden(NE - 1, c)
                if c:
                    gate_expert(NE - 1, c - 1, 0)
                else:
                    gate_expert(NE - 2, NCH - 1, 1)
                if c >= 2:
                    out_moments(c - 2)
            scale_and_offset(3, 0, CH)
            gate_expert(NE - 1, NCH - 1, 0)
            for c in range(1, NCH):
                if c >= 2:
                    out_moments(c)
                scale_and_offset(3, CH * c, CH * (c + 1))
                add_x(c - 1)
            add_x(NCH - 1)

        @block.tensor
        def _(pe):
            def three(dst, w_hi, w_lo, m_hi, m_lo, start=True, stop=True):
                pe.matmul(dst, w_hi, m_hi, start=start, stop=False)
                pe.matmul(dst, w_hi, m_lo, start=False, stop=False)
                return pe.matmul(dst, w_lo, m_hi, start=False, stop=stop)

            def transposes(n, c):
                if n:
                    pe.wait_ge(moe_in_ready, CH * (c + 1))
                else:
                    pe.wait_ge(normed_ready, c + 1)
                if n or c >= 2:
                    pe.wait_ge(nT_ready, n * NCH + c - 1)
                for j in range(CH):
                    last = pe.transpose(trans_ps[c % 2][:, j * P:(j + 1) * P], normed[:, CH * c + j, :], ident[:])
                last.then_inc(nT_psum, 1)

            def project_qk(h, b, half):
                pe.wait_ge(wqk_ready, h + 1)
                cols = slice(b * T + half * W, b * T + (half + 1) * W)
                three(shared_ps[:], wqk_hi, wqk_lo, nT_hi[:, cols], nT_lo[:, cols]).then_inc(qk_psum, 1)

            pe.wait_ge(ident_ready, 1)
            bias_flat = bias_all[:].rearrange("p h c -> p (h c)")

            def values_of_all(t):
                if t == 0:
                    pe.wait_ge(wv_split, 1)
                if t % CH == 0:
                    pe.wait_ge(nT_ready, t // CH + 1)
                for half in range(2):
                    if t >= 2:
                        pe.wait_ge(v_evac_act if half == 0 else v_evac_dve, t - 1)
                    cols, rows = slice(half * W, (half + 1) * W), slice(t * P, (t + 1) * P)
                    three(banks[(2 * t + half) % 4], nT_hi[:, rows], nT_lo[:, rows],
                          wv_hi[:, cols], wv_lo[:, cols]).then_inc(v_psum, 1)

            transposes(0, 0)
            transposes(0, 1)
            for t in range(4):
                values_of_all(t)
                if t % 2:
                    transposes(0, 2 + t // 2)
            project_qk(0, 0, 0)
            values_of_all(4)
            values_of_all(5)
            pe.wait_ge(qk_lo, 1)
            project_qk(0, 0, 1)
            for t in range(6, NB):
                values_of_all(t)
                n = t - (NB - N_TURN)
                if n >= 0:
                    if n == 0:
                        pe.wait_ge(bias_loaded, 16)
                        pe.wait_ge(ident_ready, 2)
                        pe.wait_ge(nT_ready, NCH)
                    if n >= 2:
                        pe.wait_ge(bias_turned, n - 1)
                    pe.matmul(trans_ps[n % 2][:], exchange[:], bias_flat[:, n * W:(n + 1) * W],
                              start=True, stop=True).then_inc(bias_turn_psum, 1)

            def wait_shared(h, s, last):
                uses = [u for u in SHARED_USE if u[0] < s and not (isinstance(h, int) and h == 0 and u[2] < 0)
                        and not (last and u[2] > 0)]
                if isinstance(h, int) and h == 0 and not uses:
                    pe.wait_ge(qk_lo, NC)
                    return
                _, kind, n, b, part = uses[-1] if uses else SHARED_USE[-1]
                n = h + n if uses else h - 1
                if kind == "qk":
                    pe.wait_ge(qk_lo, n * (2 * B) + 2 * b + part + 1)
                else:
                    pe.wait_ge(wo_scaled, n * (B * NC) + b * NC + part + 1)

            def scores(h, s):
                b, i = divmod(s, QB)
                if i == 0:
                    pe.wait_ge(k_copied[b], h * 16 + 16)
                if not (isinstance(h, int) and h == 0 and s < CH):
                    pe.wait_ge(probs_ready, h * S + s - i + scores_before(i))
                q = q_hl[b][:, i * P:(i + 1) * P]
                n = P * max(i + 1, 2)
                at = 0
                for end in [n] if n <= W else [W - scores_at(i), n]:
                    for part in range(2):
                        last = pe.matmul(scores_of(i)[:, at:end], q, k_hl[b][:, part, at:end],
                                         start=part == 0, stop=part == 1)
                    at = end
                last.then_inc(scores_ready, 1)

            def transpose_probs(h, s, g):
                i = s % QB
                k = group_of(s, g)
                if g == 0:
                    pe.wait_ge(probs_ready, h * S + s + 1)
                if not (isinstance(h, int) and h == 0 and k < 2):
                    pe.wait_ge(pT_ready, h * G_HEAD + k - 1)
                for j in range(CH * g, min(CH * (g + 1), i + 1)):
                    o = (j - CH * g) * P
                    last = pe.transpose(trans_ps[k % 2][:, o:o + P], probs[s % 4][:, j * P:(j + 1) * P], ident[:])
                last.then_inc(pT_psum, 1)

            def values(h, b, c, j0, j1):
                u = h * (B * NC) + b * NC + c
                nk = CH * (c + 1)
                if j0 == 0:
                    pe.wait_ge(pT_ready, h * G_HEAD + group_of(QB * b + CH * c + CH - 1, c) + 1)
                    if c == 0:
                        pe.wait_ge(v_ready, h * B + b + 1)
                    if isinstance(u, int) and u == 0:
                        pe.wait_ge(zeros_ready, 2 * NC)
                    else:
                        pe.wait_ge(oT_ready, u)
                for j in range(j0, j1):
                    q0 = min(max(0, j - CH * c), CH - 2) * P
                    for part in (pT_hi, pT_lo):
                        last = pe.matmul(out_ps[:, q0:W], v_hl[b][:, j, :], part[c][:, j, q0:W],
                                         start=j == 0 and part is pT_hi, stop=j == nk - 1 and part is pT_lo)
                if j1 == nk:
                    last.then_inc(oT_psum, 1)

            def project_out(h, b, c, j0, j1):
                if isinstance(h, int) and h == 0 and (b, c, j0) == (0, 0, 0):
                    pe.wait_ge(wo_loaded, 32)
                if j0 == 0:
                    pe.wait_ge(oT_ready, h * (B * NC) + b * NC + c + 1)
                for j in range(j0, j1):
                    last = pe.matmul(shared_ps[:, j * P:(j + 1) * P], oT[c][:, j * P:(j + 1) * P],
                                     wo[:, h, :], start=True, stop=True)
                if j1 == CH:
                    last.then_inc(wo_psum, 1)

            def fillers(h, s, last):
                first = isinstance(h, int) and h == 0
                pieces = []
                for n, at in ((h - 1, s + S), (h, s)):
                    if at >= S and first:
                        continue
                    if at in PV_SLOT:
                        b, c, j0, j1 = PV_SLOT[at]
                        pieces += [lambda n=n, b=b, c=c, j=j: values(n, b, c, j, j + 1) for j in range(j0, j1)]
                    if at in WO_SLOT:
                        b, c = WO_SLOT[at]
                        pieces.append(lambda n=n, b=b, c=c: (wait_shared(h, s, last), project_out(n, b, c, 0, 2)))
                        pieces.append(lambda n=n, b=b, c=c: project_out(n, b, c, 2, CH))
                if s in QK_SLOT:
                    nxt, b, half = QK_SLOT[s]
                    if not (nxt and last):
                        pieces.append(lambda: (wait_shared(h, s, last), project_qk(h + nxt, b, half)))
                return pieces

            def slot(h, s, carried, last):
                scores(h, s)
                pieces = fillers(h, s, last)
                n, t = (h, s - LAG_PE) if s >= LAG_PE else (h - 1, s - LAG_PE + S)
                if s >= LAG_PE or carried:
                    for g in range(GROUPS[t % QB]):
                        transpose_probs(n, t, g)
                        if pieces:
                            pieces.pop(0)()
                for piece in pieces:
                    piece()

            for r in range(2):
                pe.wait_ge((v_evac_act, v_evac_dve)[r], NB)
            for s in range(S):
                slot(0, s, False, False)
            with pe.Fori(1, H - 1) as h:
                for s in range(S):
                    slot(h, s, True, False)
            for s in range(S):
                slot(H - 1, s, True, True)
            carried_uses = sorted(t for t in WO_SLOT if t >= S)
            for s in range(S, TAIL):
                if s - LAG_PE < S:
                    for g in range(GROUPS[(s - LAG_PE) % QB]):
                        transpose_probs(H - 1, s - LAG_PE, g)
                if s in PV_SLOT:
                    values(H - 1, *PV_SLOT[s])
                if s in WO_SLOT:
                    pe.wait_ge(wo_scaled, H * B * NC - len(carried_uses) + carried_uses.index(s))
                    project_out(H - 1, *WO_SLOT[s], 0, CH)

            def logits():
                pe.wait_ge(wr_ready, 1)
                pe.wait_ge(nT_ready, 2 * NCH)
                for t in range(NB):
                    for part in (nT_hi, nT_lo):
                        last = pe.matmul(out_ps[:, 2 * E * t:2 * E * t + 4 * DH], part[:, t * P:(t + 1) * P],
                                         wqk_hl[:], start=part is nT_hi, stop=part is nT_lo)
                last.then_inc(logit_psum, 1)

            def hidden_units(e, c, i):
                for k in range(HB):
                    if not (isinstance(e, int) and e == 0 and c == 0):
                        pe.wait_ge(hidden_ready, e * (NCH * HB) + (c - 1) * HB + k + 1)
                    ws, ts = slice(k * P, (k + 1) * P), slice(c * W, (c + 1) * W)
                    three(banks[k], wfc_hi[i][:, ws], wfc_lo[i][:, ws], nT_hi[:, ts], nT_lo[:, ts])\
                        .then_inc(fc_psum, 1)

            def second_layer(e, c, i):
                pe.wait_ge(hidden_lo_ready, e * (NCH * HB) + c * HB + HB)
                if c == 0:
                    pe.wait_ge(wproj_ready, e + 1)
                if not (isinstance(e, int) and e == 0 and c < 2):
                    pe.wait_ge(gated_ready, e * NCH + c - 1)
                for k in range(HB):
                    last = three(trans_ps[c % 2][:], wproj_hi[i][:, k, :], wproj_lo[i][:, k, :],
                                 hidden_hi[c % 2][k], hidden_lo[c % 2][k], start=k == 0, stop=k == HB - 1)
                last.then_inc(moe_psum, 1)

            def expert(e, i, before):
                pe.wait_ge(wfc_ready, e + 1)
                for c in range(NCH):
                    hidden_units(e, c, i)
                    if c:
                        second_layer(e, c - 1, i)
                    else:
                        second_layer(before, NCH - 1, 1 - i)

            def transpose_gates():
                pe.wait_ge(gate_ready, 1)
                for c in range(NCH):
                    last = pe.transpose(out_ps[0:CH * E, c * P:(c + 1) * P],
                                        gate[:, CH * c:CH * (c + 1), :].rearrange("p j e -> p (j e)"), ident[:])
                last.then_inc(gate_T_psum, 1)

            for c in range(NC):
                transposes(1, c)
            pe.wait_ge(wo_scaled, H * B * NC)
            pe.wait_ge(small_loaded, 16 * 5)
            rows = NE * HB + NE
            pe.transpose(shared_ps[:, 0:rows], layer_bias[:], ident[0:rows, 0:rows]).then_inc(layer_bias_psum, 1)
            pe.wait_ge(wfc_ready, 1)
            for c in range(NC):
                pe.wait_ge(nT_ready, NCH + c + 1)
                hidden_units(0, c, 0)
            for c in range(NC, NCH):
                transposes(1, c)
            pe.wait_ge(nT_ready, 2 * NCH)
            logits()
            second_layer(0, 0, 0)
            hidden_units(0, 2, 0)
            second_layer(0, 1, 0)
            hidden_units(0, 3, 0)
            transpose_gates()
            second_layer(0, 2, 0)
            with pe.Fori(1, NE - 2, 2) as e:
                expert(e, 1, e - 1)
                expert(e + 1, 0, e)

            def transpose_out(c):
                pe.wait_ge(moe_added, (NE - 2) * NCH + c + 1)
                for j in range(CH):
                    t = CH * c + j
                    last = pe.transpose(moe_out[c][:, j * P:(j + 1) * P],
                                        acc_T[:, t * P:(t + 1) * P], ident[:])
                last.then_inc(moe_out_psum, 1)

            expert(NE - 2, 1, NE - 3)
            pe.wait_ge(wfc_ready, NE)
            for c in range(NCH):
                hidden_units(NE - 1, c, 0)
                if c >= 2:
                    transpose_out(c - 2)
                if c:
                    second_layer(NE - 1, c - 1, 0)
                else:
                    second_layer(NE - 2, NCH - 1, 1)
            second_layer(NE - 1, NCH - 1, 0)
            for c in (NCH - 2, NCH - 1):
                transpose_out(c)


_INS = ["L0_attn_x", "L0_attn_Wq", "L0_attn_Wk", "L0_attn_Wv", "L0_attn_Wo", "L0_attn_bo",
        "L0_attn_rel_pos_bias", "L0_ffn_Wfc_s", "L0_ffn_bfc_s", "L0_ffn_Wproj_s", "L0_ffn_bproj_s",
        "L0_ffn_Wr", "L0_ffn_Wfc", "L0_ffn_bfc", "L0_ffn_Wproj", "L0_ffn_bproj"]


def kernel(**inputs):
    import numpy as _np
    import concourse.bacc as _bacc
    from concourse import mybir as _mybir
    from concourse.bass_utils import run_bass_kernel_spmd as _run

    nc = _bacc.Bacc("TRN2", target_bir_lowering=False, num_devices=1)
    arrays, args = {}, []
    for name in _INS:
        a = _np.ascontiguousarray(inputs[name])
        arrays[f"in_{name}"] = a
        args.append(nc.dram_tensor(f"in_{name}", a.shape, _mybir.dt.from_np(a.dtype), kind="ExternalInput").ap())
    shape = inputs["L0_attn_x"].shape
    args.append(nc.dram_tensor("out_0", shape, _mybir.dt.float32, kind="ExternalOutput").ap())
    transformer_block(nc, *args)
    r = _run(nc, [arrays], core_ids=[0])
    return r.results[0]["out_0"]
```
